# Optimizing a Trainium2 kernel written in Bass

```python
import numpy as np
import jax
import jax.numpy as jnp

def _softmax(x, axis=-1):
    return jax.nn.softmax(x, axis=axis)

def _gelu(x):
    return jax.nn.gelu(x, approximate=True)

def _silu(x):
    return jax.nn.silu(x)

def _sigmoid(x):
    return jax.nn.sigmoid(x)

def _layernorm(x, axis=-1, eps=1e-05):
    m = jnp.mean(x, axis=axis, keepdims=True)
    v = jnp.var(x, axis=axis, keepdims=True)
    return (x - m) / jnp.sqrt(v + eps)

def _scatter_add(tgt, idx, src, axis=0):
    return tgt.at[idx].add(src)

def _segment_sum(src, seg, n):
    return jax.ops.segment_sum(src, seg, n)
kernel_name = 'mk_prb_d1_jaxref_r8_0bf9f9'

def setup_inputs(seed: int=0):
    np.random.seed(seed)
    _w = jnp.asarray

    def _L0_attn_setup():
        import jax, jax.numpy as jnp
        import numpy as np
        H = 512
        D = 1024
        N = 16
        K = 4
        R = 32
        BATCH = 1
        L = 256
        EPS = 1e-06

        def _rmsnorm(x, w):
            return x * jax.lax.rsqrt(jnp.mean(x * x, axis=-1, keepdims=True) + EPS) * w
        key = jax.random.key(seed)
        ks = jax.random.split(key, 10)
        s = 0.02
        return {'hidden_states': jax.random.normal(ks[0], (BATCH, L, H), jnp.float32), 'W_in': jax.random.normal(ks[1], (2 * D, H), jnp.float32) * s, 'conv_w': jax.random.normal(ks[2], (D, K), jnp.float32) * s, 'conv_b': jax.random.normal(ks[3], (D,), jnp.float32) * s, 'Wx': jax.random.normal(ks[4], (R + 2 * N, D), jnp.float32) * s, 'dt_ln_w': jnp.ones((R,), jnp.float32), 'b_ln_w': jnp.ones((N,), jnp.float32), 'c_ln_w': jnp.ones((N,), jnp.float32), 'Wdt': jax.random.normal(ks[5], (D, R), jnp.float32) * s, 'dt_bias': jax.random.normal(ks[6], (D,), jnp.float32) * s, 'A': -jnp.exp(jax.random.normal(ks[7], (D, N), jnp.float32) * 0.5), 'D_param': jnp.ones((D,), jnp.float32), 'W_out': jax.random.normal(ks[8], (H, D), jnp.float32) * s}
    _L0_attn_in = _L0_attn_setup()

    def _L0_ffn_setup():
        import jax, jax.numpy as jnp
        import numpy as np
        HIDDEN = 512
        INTER = 1376
        GROUP = 128
        B, S = (4, 256)
        NIB = jnp.uint32(15)

        def _pack_rows(nib):
            r = nib.reshape(-1, 8, nib.shape[-1])
            shifts = (jnp.arange(8, dtype=jnp.uint32) * 4)[None, :, None]
            return jnp.sum(r << shifts, axis=1, dtype=jnp.uint32)

        def _pack_cols(nib):
            r = nib.reshape(nib.shape[0], -1, 8)
            shifts = (jnp.arange(8, dtype=jnp.uint32) * 4)[None, None, :]
            return jnp.sum(r << shifts, axis=2, dtype=jnp.uint32)

        def _dequant(qw, qz, sc, g_idx):
            shifts = jnp.arange(8, dtype=jnp.uint32) * 4
            wq = qw[:, None, :] >> shifts[None, :, None] & NIB
            wq = wq.reshape(-1, qw.shape[1]).astype(jnp.float32)
            zq = qz[:, :, None] >> shifts[None, None, :] & NIB
            zq = zq.reshape(qz.shape[0], -1).astype(jnp.float32) + 1.0
            return sc[g_idx] * (wq - zq[g_idx])
        key = jax.random.key(seed)
        ks = jax.random.split(key, 7)
        n_groups = HIDDEN // GROUP
        n_groups_d = INTER // GROUP
        x = jax.random.normal(ks[0], (B, S, HIDDEN), jnp.float32)
        nib_w_gu = jax.random.randint(ks[1], (HIDDEN, 2 * INTER), 0, 16).astype(jnp.uint32)
        nib_z_gu = jax.random.randint(ks[2], (n_groups, 2 * INTER), 0, 15).astype(jnp.uint32)
        qweight_gu = _pack_rows(nib_w_gu)
        qzeros_gu = _pack_cols(nib_z_gu)
        scales_gu = jax.random.uniform(ks[3], (n_groups, 2 * INTER), jnp.float32, 0.005, 0.02)
        g_idx_gu = jnp.arange(HIDDEN, dtype=jnp.int32) // GROUP
        nib_w_d = jax.random.randint(ks[4], (INTER, HIDDEN), 0, 16).astype(jnp.uint32)
        nib_z_d = jax.random.randint(ks[5], (n_groups_d, HIDDEN), 0, 15).astype(jnp.uint32)
        qweight_down = _pack_rows(nib_w_d)
        qzeros_down = _pack_cols(nib_z_d)
        scales_down = jax.random.uniform(ks[6], (n_groups_d, HIDDEN), jnp.float32, 0.005, 0.02)
        g_idx_down = jnp.arange(INTER, dtype=jnp.int32) // GROUP
        return {'x': x, 'qweight_gu': qweight_gu, 'qzeros_gu': qzeros_gu, 'scales_gu': scales_gu, 'g_idx_gu': g_idx_gu, 'qweight_down': qweight_down, 'qzeros_down': qzeros_down, 'scales_down': scales_down, 'g_idx_down': g_idx_down}
    _L0_ffn_in = _L0_ffn_setup()
    _d = {'L0_attn_hidden_states': _L0_attn_in['hidden_states'], 'L0_attn_W_in': _L0_attn_in['W_in'], 'L0_attn_conv_w': _L0_attn_in['conv_w'], 'L0_attn_conv_b': _L0_attn_in['conv_b'], 'L0_attn_Wx': _L0_attn_in['Wx'], 'L0_attn_dt_ln_w': _L0_attn_in['dt_ln_w'], 'L0_attn_b_ln_w': _L0_attn_in['b_ln_w'], 'L0_attn_c_ln_w': _L0_attn_in['c_ln_w'], 'L0_attn_Wdt': _L0_attn_in['Wdt'], 'L0_attn_dt_bias': _L0_attn_in['dt_bias'], 'L0_attn_A': _L0_attn_in['A'], 'L0_attn_D_param': _L0_attn_in['D_param'], 'L0_attn_W_out': _L0_attn_in['W_out'], 'L0_ffn_qweight_gu': _L0_ffn_in['qweight_gu'], 'L0_ffn_qzeros_gu': _L0_ffn_in['qzeros_gu'], 'L0_ffn_scales_gu': _L0_ffn_in['scales_gu'], 'L0_ffn_g_idx_gu': _L0_ffn_in['g_idx_gu'], 'L0_ffn_qweight_down': _L0_ffn_in['qweight_down'], 'L0_ffn_qzeros_down': _L0_ffn_in['qzeros_down'], 'L0_ffn_scales_down': _L0_ffn_in['scales_down'], 'L0_ffn_g_idx_down': _L0_ffn_in['g_idx_down']}
    _x0 = _d['L0_attn_hidden_states']
    _d['L0_attn_hidden_states'] = jax.random.normal(jax.random.fold_in(jax.random.key(seed), 1), (2, 1024, 512), dtype=_x0.dtype)
    del _x0
    return _d

def reference(L0_attn_hidden_states, L0_attn_W_in, L0_attn_conv_w, L0_attn_conv_b, L0_attn_Wx, L0_attn_dt_ln_w, L0_attn_b_ln_w, L0_attn_c_ln_w, L0_attn_Wdt, L0_attn_dt_bias, L0_attn_A, L0_attn_D_param, L0_attn_W_out, L0_ffn_qweight_gu, L0_ffn_qzeros_gu, L0_ffn_scales_gu, L0_ffn_g_idx_gu, L0_ffn_qweight_down, L0_ffn_qzeros_down, L0_ffn_scales_down, L0_ffn_g_idx_down):

    def _L0_attn_ref(hidden_states, W_in, conv_w, conv_b, Wx, dt_ln_w, b_ln_w, c_ln_w, Wdt, dt_bias, A, D_param, W_out):
        import jax, jax.numpy as jnp
        import numpy as np
        H = 512
        D = 1024
        N = 16
        K = 4
        R = 32
        BATCH = 1
        L = 256
        EPS = 1e-06

        def _rmsnorm(x, w):
            return x * jax.lax.rsqrt(jnp.mean(x * x, axis=-1, keepdims=True) + EPS) * w
        proj = hidden_states @ W_in.T
        u, gate = jnp.split(proj, 2, axis=-1)
        x = jnp.transpose(u, (0, 2, 1))
        x = jax.lax.conv_general_dilated(x, conv_w[:, None, :], window_strides=(1,), padding=[(K - 1, 0)], dimension_numbers=('NCH', 'OIH', 'NCH'), feature_group_count=D)
        u = jax.nn.silu(jnp.transpose(x, (0, 2, 1)) + conv_b)
        ssm_p = u @ Wx.T
        dt, Bm, Cm = jnp.split(ssm_p, [R, R + N], axis=-1)
        dt = _rmsnorm(dt, dt_ln_w)
        Bm = _rmsnorm(Bm, b_ln_w)
        Cm = _rmsnorm(Cm, c_ln_w)
        delta = jax.nn.softplus(dt @ Wdt.T + dt_bias)

        def step(state, xs):
            d_t, B_t, C_t, u_t = xs
            dA = jnp.exp(d_t[..., None] * A)
            state = dA * state + (d_t * u_t)[..., None] * B_t[:, None, :]
            y_t = jnp.einsum('bdn,bn->bd', state, C_t)
            return (state, y_t)
        init = jnp.zeros((hidden_states.shape[0], D, N), hidden_states.dtype)
        xs = (jnp.swapaxes(delta, 0, 1), jnp.swapaxes(Bm, 0, 1), jnp.swapaxes(Cm, 0, 1), jnp.swapaxes(u, 0, 1))
        _, ys = jax.lax.scan(step, init, xs)
        y = jnp.swapaxes(ys, 0, 1) + u * D_param
        y = y * jax.nn.silu(gate)
        return y @ W_out.T

    def _L0_ffn_ref(x, qweight_gu, qzeros_gu, scales_gu, g_idx_gu, qweight_down, qzeros_down, scales_down, g_idx_down):
        import jax, jax.numpy as jnp
        import numpy as np
        HIDDEN = 512
        INTER = 1376
        GROUP = 128
        B, S = (4, 256)
        NIB = jnp.uint32(15)

        def _pack_rows(nib):
            r = nib.reshape(-1, 8, nib.shape[-1])
            shifts = (jnp.arange(8, dtype=jnp.uint32) * 4)[None, :, None]
            return jnp.sum(r << shifts, axis=1, dtype=jnp.uint32)

        def _pack_cols(nib):
            r = nib.reshape(nib.shape[0], -1, 8)
            shifts = (jnp.arange(8, dtype=jnp.uint32) * 4)[None, None, :]
            return jnp.sum(r << shifts, axis=2, dtype=jnp.uint32)

        def _dequant(qw, qz, sc, g_idx):
            shifts = jnp.arange(8, dtype=jnp.uint32) * 4
            wq = qw[:, None, :] >> shifts[None, :, None] & NIB
            wq = wq.reshape(-1, qw.shape[1]).astype(jnp.float32)
            zq = qz[:, :, None] >> shifts[None, None, :] & NIB
            zq = zq.reshape(qz.shape[0], -1).astype(jnp.float32) + 1.0
            return sc[g_idx] * (wq - zq[g_idx])
        w_gu = _dequant(qweight_gu, qzeros_gu, scales_gu, g_idx_gu)
        inter = jnp.einsum('bsh,hf->bsf', x, w_gu)
        gate, up = (inter[..., :INTER], inter[..., INTER:])
        h = jax.nn.silu(gate) * up
        w_d = _dequant(qweight_down, qzeros_down, scales_down, g_idx_down)
        return jnp.einsum('bsf,fh->bsh', h, w_d)
    x = L0_attn_hidden_states
    xn = _layernorm(x, axis=-1)
    x = x + _L0_attn_ref(xn, L0_attn_W_in, L0_attn_conv_w, L0_attn_conv_b, L0_attn_Wx, L0_attn_dt_ln_w, L0_attn_b_ln_w, L0_attn_c_ln_w, L0_attn_Wdt, L0_attn_dt_bias, L0_attn_A, L0_attn_D_param, L0_attn_W_out) + _L0_ffn_ref(xn, L0_ffn_qweight_gu, L0_ffn_qzeros_gu, L0_ffn_scales_gu, L0_ffn_g_idx_gu, L0_ffn_qweight_down, L0_ffn_qzeros_down, L0_ffn_scales_down, L0_ffn_g_idx_down)
    return x

_drawn_inputs = setup_inputs


def setup_inputs(seed=0):
    import zlib

    import numpy as np

    out = dict(_drawn_inputs(seed))
    spreads = {'L0_attn_dt_ln_w': (1.0, 0.6),
     'L0_attn_b_ln_w': (1.0, 0.6),
     'L0_attn_c_ln_w': (1.0, 0.6),
     'L0_attn_D_param': (1.0, 0.6)}
    factors = {'L0_attn_W_in': 8.0,
     'L0_attn_conv_w': 8.0,
     'L0_attn_conv_b': 8.0,
     'L0_attn_Wx': 8.0,
     'L0_attn_Wdt': 8.0,
     'L0_attn_dt_bias': 8.0,
     'L0_attn_A': 8.0,
     'L0_attn_W_out': 8.0,
     'L0_ffn_scales_down': 3.243}
    for name, (base, spread) in spreads.items():
        noise = np.random.default_rng([zlib.crc32(name.encode()), seed]).standard_normal(out[name].shape)
        drawn = base * np.exp(spread * noise) if base else spread * noise
        out[name] = jnp.asarray(drawn.astype(out[name].dtype))
    for name, factor in factors.items():
        out[name] = (out[name] * factor).astype(out[name].dtype)
    return out
```

```python
from contextlib import ExitStack

import concourse.bass as bass
from concourse import mybir

ALU = mybir.AluOpType
ACT = mybir.ActivationFunctionType
F32 = mybir.dt.float32
F32R = mybir.dt.float32r
U32 = mybir.dt.uint32
I32 = mybir.dt.int32

P = 128
T = 512
HID = 512
KT = HID // P
D = 1024
NC = D // P
N = 16
R = 32
XP = R + 2 * N
TAPS = 4
HALO = TAPS - 1
F = 1376
NF = -(-F // P)
GROUP = 128
G_GU = HID // GROUP
G_D = F // GROUP
EPS_LN = 1e-5
EPS_RMS = 1e-6

PAIR = 2
SPC = N // PAIR
STEPS = NC * SPC
FIRST = 0

NA, NBR = 4, 3
NDA, NHB = 2, 4
NGATE = 3
NCV = 3

FFN_STEP = [(7 * j) // 2 for j in range(NF)]
DOWN_STEP = [s + 4 for s in FFN_STEP]
GATE_STEP = [6 * c + 2 for c in range(NC)]
DTZ_STEP = [2 * SPC * q - 5 for q in range(1, NC // 2)]
RES_STEP = [2, 2, 3, 3]
XT_STEP = [45, 45, 46, 46]
U_STEP = [47 + (4 * c) // 3 for c in range(NC)]
WX_STEP = [s + 5 for s in U_STEP]
MS_STEP = 62
WOUT_STEP = [SPC * c + 12 for c in range(NC - 1)] + [STEPS]


def at(steps, s):
    return [n for n, x in enumerate(steps) if x == s]


def width(j):
    return min(P, F - j * P)


def psum_order():
    order = []
    for s in range(STEPS + 1):
        for j in at(FFN_STEP, s):
            order += [("g", j), ("up", j)]
        order += [("gate", c) for c in at(GATE_STEP, s)]
        for q in at(DTZ_STEP, s):
            order += [("dtz", 2 * q + 2), ("dtz", 2 * q + 3)]
        order += [("xt", t) for t in at(XT_STEP, s)]
        order += [("u", c) for c in at(U_STEP, s)]
        if s == MS_STEP:
            order.append(("ms", 0))
    return order + [("dtz", 0), ("dtz", 1)]


FIRST_ORDER = [("xt", t) for t in range(KT)] + [("u", c) for c in range(NC)] + [("ms", 0), ("dtz", 0), ("dtz", 1)]
BLOCK_ORDER = psum_order()


def ring_a_order():
    order = []
    for s in range(STEPS + 1):
        order += [("gate", c) for c in at(GATE_STEP, s)]
        order += [("u", c) for c in at(U_STEP, s)]
        order += [("wout", c) for c in at(WOUT_STEP, s)]
    return order


def ring_b_order():
    order = []
    for s in range(STEPS + 1):
        for j in at(FFN_STEP, s):
            order += [("g", j), ("up", j)]
        order += [("down", j) for j in at(DOWN_STEP, s)]
    return order


RING_A, RING_B = ring_a_order(), ring_b_order()
UNIT = {("u", c): c for c in range(NC)}
UNIT |= {("gate", c): NC + c for c in range(NC)}
UNIT |= {("wout", c): 2 * NC + c for c in range(NC)}
UNIT |= {("g", j): 3 * NC + 2 * j for j in range(NF)}
UNIT |= {("up", j): 3 * NC + 2 * j + 1 for j in range(NF)}
UNIT |= {("down", j): 3 * NC + 2 * NF + j for j in range(NF)}
UNITS = len(UNIT)
KIND = {n: kind for kind, n in UNIT.items()}

VEC_LINKS = 102
ACT_LINKS = 4


def build(nc, x, W_in, conv_w, conv_b, Wx, dt_ln_w, b_ln_w, c_ln_w, Wdt, dt_bias, A, D_param, W_out,
          qw_gu, qz_gu, sc_gu, idx_gu, qw_d, qz_d, sc_d, idx_d, consts, out):
    tokens = x.shape[0] * x.shape[1]
    BLOCKS = tokens // T
    PER_SEQ = x.shape[1] // T
    assert BLOCKS > 0
    assert len(RING_A) % NA == 0 and len(RING_B) % NBR == 0 and NC % NA == 0

    x_tok = x.rearrange("b (k t p) h -> (b k) t p h", p=P, t=T // P)
    out_tok = out.rearrange("b (k t p) h -> (b k) t p h", p=P, t=T // P)

    ctx = ExitStack()
    with ctx:
        def sb(name, shape, dt=F32):
            return ctx.enter_context(nc.sbuf_tensor(name, shape, dt))

        def sem(name):
            return ctx.enter_context(nc.semaphore(name))

        units = nc.dram_tensor("weight_units", [UNITS, P, 2 * T], F32, kind="Internal").ap()
        bc_dram = nc.dram_tensor("bc_rows", [2 * N, T], F32, kind="Internal").ap()

        bc_all = sb("bc_all", [P, 2 * N * T])
        B_bc = bc_all[:, 0:N * T].rearrange("p (n t) -> p n t", n=N)
        C_bc = bc_all[:, N * T:2 * N * T].rearrange("p (n t) -> p n t", n=N)
        ring_a = sb("ring_a", [P, NA, 2, T], F32R)
        ring_b = sb("ring_b", [P, NBR, 2, T], F32R)
        ssm = sb("ssm", [P, (NDA + NHB) * PAIR * T])
        dA = ssm[:, 0:NDA * PAIR * T].rearrange("p (b k t) -> p b k t", b=NDA, k=PAIR)
        hb = ssm[:, NDA * PAIR * T:].rearrange("p (b k t) -> p b k t", b=NHB, k=PAIR)
        xT = sb("xT", [P, 2, KT, T], F32R)
        u = sb("u", [P, NC, T])
        gate = sb("gate", [P, NGATE, T])
        ffn_e = sb("ffn_e", [P, T])
        ffn_g = sb("ffn_g", [P, T])
        ffn_u = sb("ffn_u", [P, T])
        h_hl = sb("h_hl", [P, 2, T], F32R)
        y_hl = sb("y_hl", [P, 2, T], F32R)
        u_raw = sb("u_raw", [P, NCV, T + HALO])
        conv = sb("conv", [P, NCV, T])
        e_cg = sb("e_cg", [P, T])
        gate_e = sb("gate_e", [P, T])
        sp_z = sb("sp_z", [P, 2, T])
        sp_l = sb("sp_l", [P, 2, T])
        delta = sb("delta", [P, 4, T])
        du = sb("du", [P, 2, T])
        ud = sb("ud", [P, T])
        tok = sb("tok", [P, 2, HID])
        xdn = sb("xdn", [P, T])
        WxT = sb("WxT", [P, NC, XP])
        WdtT = sb("WdtT", [P, D])
        A_sb = sb("A_sb", [P, NC, N])
        cst = sb("cst", [P, consts.shape[1]])
        ident = cst[:, 0:P]
        mean_m = cst[:, P:2 * P]
        row_col = cst[:, 2 * P:2 * P + 1]
        minus_half = cst[:, 2 * P + 1:2 * P + 2]
        lim0 = 2 * P + 2
        nlim = BLOCKS + 1
        shift = sb("shift", [P, 1], U32)
        cw = sb("cw", [P, NC, TAPS])
        cb = sb("cb", [P, NC])
        dtb = sb("dtb", [P, NC])
        dpar = sb("dpar", [P, NC])
        lnw = sb("lnw", [P, 1])
        carry = sb("carry", [P, NC * N])
        halo = sb("halo", [P, NC, HALO])
        st6 = sb("st6", [P, KT, 6])
        mv = sb("mv", [P, KT, 2])
        rstd = sb("rstd", [P, KT])
        nmr = sb("nmr", [P, KT])

        ps = ctx.enter_context(nc.psum_tensor("ps", [P, 8, T], F32))
        acc = ps[:, 0:4, :]
        PB = [ps[:, 4, :], ps[:, 5, :]]
        Y = ps[:, 6, :]
        M = ps[:, 7, :]

        const_full = sem("const_full")
        zeroed = sem("zeroed")
        win_full = sem("win_full"); wout_full = sem("wout_full"); wsmall_full = sem("wsmall_full")
        words_full = sem("words_full"); dwords_full = [sem(f"dwords_full{b}") for b in range(4)]
        scale_full = sem("scale_full"); dscale_full = sem("dscale_full")
        prep_vec = sem("prep_vec"); scale_split = sem("scale_split"); dscale_split = sem("dscale_split")
        prep_mm = sem("prep_mm"); prep_hi = sem("prep_hi"); prep_w = sem("prep_w"); prep_lo = sem("prep_lo")
        small_t = sem("small_t"); small_copied = sem("small_copied")
        stored = [sem("stored0"), sem("stored1")]
        a_full = [sem(f"a_full{k}") for k in range(NA)]
        b_full = [sem(f"b_full{k}") for k in range(NBR)]
        wx_done = sem("wx_done")
        p_full = sem("p_full"); p_read = [sem("p_read0"), sem("p_read1")]
        exp_done = sem("exp_done"); dbu_done = sem("dbu_done"); scan_done = sem("scan_done")
        p_done = sem("p_done"); nsum_done = sem("nsum_done")
        bb_full = [sem(f"bb_full{g}") for g in range(SPC)]
        cb_full = [sem(f"cb_full{g}") for g in range(SPC)]
        bc_stored = sem("bc_stored")
        sp_ready = sem("sp_ready"); delta_ready = sem("delta_ready"); du_ready = sem("du_ready")
        ud_ready = sem("ud_ready"); y_added = sem("y_added"); y_gated = sem("y_gated")
        yh_ready = sem("yh_ready"); yl_ready = sem("yl_ready"); wout_done = sem("wout_done")
        gate_ready = sem("gate_ready")
        h_ready = sem("h_ready"); hh_ready = sem("hh_ready"); hl_ready = sem("hl_ready")
        down_done = sem("down_done")
        ln_full = sem("ln_full"); ln_var = sem("ln_var"); ln_pow = sem("ln_pow"); ms_pow = sem("ms_pow")
        ln_stats = sem("ln_stats"); ln_norm = sem("ln_norm")
        xh_ready = sem("xh_ready"); xt_ready = sem("xt_ready")
        cv_ready = sem("cv_ready"); ue_ready = sem("ue_ready"); u_ready = sem("u_ready")
        sq_ready = sem("sq_ready"); xdn_ready = sem("xdn_ready")
        tok_full = [sem("tok_full0"), sem("tok_full1")]
        res_done = sem("res_done"); out_evac = sem("out_evac")
        tok_out = [sem("tok_out0"), sem("tok_out1")]
        vec_link = sem("vec_link"); act_link = sem("act_link")

        def step_no(i, s):
            return STEPS * i + (STEPS + s + 1)

        def psum_use(i, kind):
            order = FIRST_ORDER if i is None else BLOCK_ORDER
            pos = order.index(kind)
            bank = pos % 2
            nth = pos // 2 + 1
            if i is None:
                return bank, pos + 1, nth
            per = (len(BLOCK_ORDER) + 1 - bank) // 2
            before = (len(FIRST_ORDER) + 1 - bank) // 2
            return (bank, len(BLOCK_ORDER) * i + (len(FIRST_ORDER) + pos + 1),
                    per * i + (before + nth))

        def psum_free(eng, i, kind):
            bank, _, nth = psum_use(i, kind)
            if i is not None or nth > 1:
                eng.wait_ge(p_read[bank], nth - 1)

        def a_use(i, kind):
            if i is None:
                return kind[1] % NA, kind[1]
            k = RING_A.index(kind)
            return k % NA, len(RING_A) * i + (NC + k)

        def fill_count(i, kind):
            if i is None:
                return kind[1] // NA + 1
            return len(RING_A) // NA * i + (NC // NA + RING_A.index(kind) // NA + 1)

        WORDS = 2 * F * KT
        win_tiles = [ssm[:, 0:NC * HID].rearrange("p (r h) -> p r h", r=NC), u]
        words = bc_all[:, 0:WORDS].bitcast(U32).rearrange("p (k f) -> p k f", k=KT)
        wout_nat = bc_all[:, WORDS:WORDS + HID // P * D].rearrange("p (f d) -> p f d", f=HID // P)
        dwords = bc_all[:, WORDS:WORDS + 4 * HID].bitcast(U32).rearrange("p (b h) -> p b h", b=4)
        didx = bc_all[0:G_D, WORDS + 4 * HID:WORDS + 4 * HID + F]
        sc_raw = ssm[0:G_GU, 0:2 * F]
        z_int = ssm[0:G_GU, 2 * F:4 * F].bitcast(U32)
        qz_raw = ssm[0:G_GU, 4 * F:4 * F + F // 4].bitcast(U32)
        gidx = ffn_e[0:G_GU, :]
        dsc_raw = ffn_u[0:G_D, :]
        dz_int = e_cg[0:G_D, :].bitcast(U32)
        dqz_raw = tok[0:G_D, 0, 0:HID // 8].bitcast(U32)
        wx_nat = delta[0:XP, 0:2, :].rearrange("p a t -> p (a t)")
        wdt_nat = du[:, 0, 0:NC * R].rearrange("p (c r) -> p c r", c=NC)
        LOW = 32
        xT_flat = xT[:].rearrange("p a k t -> p (a k t)")
        ra_flat = ring_a[:].rearrange("p s a t -> p (s a t)")
        rb_flat = ring_b[:].rearrange("p s a t -> p (s a t)")
        sc_parts, z_rows, pick = xT_flat[:, 0:2 * F], rb_flat[:, 0:2 * F], h_hl[:, 0, :]
        dsc_parts, dz_rows, dpick = y_hl[:, 0, :], h_hl[:, 1, :], ra_flat[:, 0:F]
        stage = [xT_flat[:, 3 * 2 * T:4 * 2 * T].rearrange("p (a t) -> p a t", a=2),
                 ra_flat[:, 3 * 2 * T:4 * 2 * T].rearrange("p (a t) -> p a t", a=2)]
        w_int = [sp_z[:, 0, :], sp_l[:, 0, :]]
        ZEROED = 10
        lnx = [ffn_e, ffn_g, ffn_u, e_cg]
        DEQ = 3 * NC

        def unit_view(tile, n):
            kind, k = KIND[n]
            if kind in ("g", "up") and width(k) < P:
                return tile.rearrange("p a (k f) -> p a k f", k=KT)[:, :, :, 0:width(k)]
            if kind == "down":
                return tile[0:width(k)]
            return tile

        def unit_dram(n):
            return unit_view(units[n].rearrange("p (a t) -> p a t", a=2), n)

        def unit_used(sp, i, kind):
            if kind[0] == "down":
                sp.wait_ge(down_done, NF * i + (kind[1] + 1))
            elif kind[0] == "wout":
                sp.wait_ge(wout_done, NC * i + (kind[1] + 1))
            else:
                sp.wait_ge(p_full, psum_use(i, kind)[1])

        def ring_b_step(kind):
            return (DOWN_STEP if kind[0] == "down" else FFN_STEP)[kind[1]]

        def ring_a_step(kind):
            return {"gate": GATE_STEP, "u": U_STEP, "wout": WOUT_STEP}[kind[0]][kind[1]]

        def load_down_words(sp, j):
            for r in range(8):
                sp.dma_start(dwords[r:width(j):8, j % 4, :],
                             qw_d[16 * j:16 * j + width(j) // 8, :]).then_inc(dwords_full[j % 4], 16)

        def out_project(pe, into_acc, i, c):
            slot, _ = a_use(i, ("wout", c))
            pe.wait_ge(a_full[slot], 16 * fill_count(i, ("wout", c)))
            pe.wait_ge(yl_ready, NC * i + (c + 1))
            into_acc(ring_a, slot, P, y_hl, c == NC - 1, wout_done)

        def y_high(i, c):
            nc.scalar.wait_ge(y_gated, NC * i + (c + 1))
            nc.scalar.wait_ge(wout_done, NC * i + c)
            nc.scalar.copy(y_hl[:, 0, :], ud[:]).then_inc(yh_ready, 1)

        def y_low(i, c):
            nc.gpsimd.wait_ge(yh_ready, NC * i + (c + 1))
            nc.gpsimd.tensor_tensor(y_hl[:, 1, :], ud[:], y_hl[:, 0, :].bitcast(F32),
                                    ALU.subtract).then_inc(yl_ready, 1)

        block = ctx.enter_context(nc.Block())

        @block.sync
        def _(sp):
            win_v = W_in.rearrange("(r p) h -> p r h", p=P)
            sp.dma_start(win_tiles[0], win_v[:, 0:NC, :]).then_inc(win_full, 16)
            sp.dma_start(cst[:], consts).then_inc(const_full, 16)
            sp.dma_start(u[:], win_v[:, NC:2 * NC, :]).then_inc(win_full, 16)
            sp.dma_start(wout_nat, W_out.rearrange("(f p) d -> p f d", p=P)).then_inc(wout_full, 16)
            sp.dma_start(wx_nat, Wx).then_inc(wsmall_full, 16)
            sp.dma_start(wdt_nat, Wdt.rearrange("(c p) r -> p c r", p=P)).then_inc(wsmall_full, 16)
            sp.dma_start(cw[:], conv_w.rearrange("(c p) k -> p c k", p=P)).then_inc(const_full, 16)
            for tile, vec in ((cb, conv_b), (dtb, dt_bias), (dpar, D_param)):
                sp.dma_start(tile[:], vec.rearrange("(c p) -> p c", p=P),
                             allow_slow_non_contiguous=True).then_inc(const_full, 16)
            sp.dma_start(A_sb[:], A.rearrange("(c p) n -> p c n", p=P)).then_inc(const_full, 16)
            for lo, hi, vec in ((0, R, dt_ln_w), (R, R + N, b_ln_w), (R + N, XP, c_ln_w)):
                sp.dma_start(lnw[lo:hi, :], vec.unsqueeze(1)).then_inc(const_full, 16)
            sp.dma_start(gidx.bitcast(I32), idx_gu.unsqueeze(0).broadcast_to([G_GU, HID])).then_inc(scale_full, 16)
            sp.dma_start(dsc_raw, sc_d).then_inc(dscale_full, 16)
            sp.dma_start(dqz_raw, qz_d).then_inc(dscale_full, 16)
            for r in range(8):
                sp.dma_start(words[r:P:8, :, :],
                             qw_gu.rearrange("(k w) f -> w k f", k=KT)).then_inc(words_full, 16)
            for n in range(UNITS):
                if n == NC:
                    sp.wait_ge(prep_mm, NC)
                    sp.dma_start(sc_raw, sc_gu).then_inc(scale_full, 16)
                    sp.dma_start(qz_raw, qz_gu).then_inc(scale_full, 16)
                if n == DEQ + 1:
                    sp.wait_ge(prep_mm, DEQ)
                    sp.dma_start(didx.bitcast(I32), idx_d.unsqueeze(0).broadcast_to([G_D, F])).then_inc(dscale_full, 16)
                    for j in range(4):
                        load_down_words(sp, j)
                if KIND[n][0] == "down" and 4 <= KIND[n][1] + 2 < NF:
                    j = KIND[n][1] + 2
                    sp.wait_ge(prep_w, n - DEQ - 1)
                    load_down_words(sp, j)
                sp.wait_ge(prep_lo, n + 1)
                sp.dma_start(unit_dram(n), unit_view(stage[n % 2].bitcast(F32), n)).then_inc(stored[n % 2], 16)
            sp.wait_ge(stored[0], 16 * ((UNITS + 1) // 2))
            sp.wait_ge(stored[1], 16 * (UNITS // 2))

            def load_a(i, kind):
                slot, use = a_use(i, kind)
                if i is None:
                    if use >= NA:
                        sp.wait_ge(p_full, psum_use(None, ("u", use - NA))[1])
                else:
                    k = RING_A.index(kind)
                    if k >= NA:
                        unit_used(sp, i, RING_A[k - NA])
                    elif RING_A[k - NA][0] == "wout":
                        sp.wait_ge(wout_done, NC * i)
                        sp.wait_ge(p_full, len(BLOCK_ORDER) * i + psum_use(None, ("u", NC - 1))[1])
                    else:
                        sp.wait_ge(p_full, len(BLOCK_ORDER) * i + psum_use(None, ("u", NC - 1))[1])
                n = UNIT[kind]
                sp.dma_start(unit_view(ring_a[:, slot].bitcast(F32), n), unit_dram(n)).then_inc(a_full[slot], 16)

            def load_x(m, block_no):
                for t in range(KT):
                    sp.dma_start(lnx[t][:], x_tok[block_no, t]).then_inc(ln_full, 16)

            load_x(FIRST, 0)
            for c in range(NC):
                load_a(None, ("u", c))
            with sp.Fori(0, BLOCKS) as i:
                for s in range(STEPS + 1):
                    for n, kind in enumerate(RING_B):
                        if ring_b_step(kind) == s:
                            if n < NBR:
                                sp.wait_ge(down_done, NF * i)
                            else:
                                unit_used(sp, i, RING_B[n - NBR])
                            sp.dma_start(unit_view(ring_b[:, n % NBR].bitcast(F32), UNIT[kind]),
                                         unit_dram(UNIT[kind])).then_inc(b_full[n % NBR], 16)
                    for kind in RING_A:
                        if ring_a_step(kind) == s:
                            load_a(i, kind)
                    for t in at(RES_STEP, s):
                        if t < 2:
                            sp.wait_ge(tok_out[t % 2], 32 * i)
                        else:
                            sp.wait_ge(res_done, KT * i + (t - 1))
                        sp.dma_start(tok[:, t % 2, :], x_tok[i, t]).then_inc(tok_full[t % 2], 16)
                    if s == XT_STEP[0] - 4:
                        following = sp.snap((i + 1) % BLOCKS)
                        sp.wait_ge(hl_ready, NF * i + NF)
                        load_x(i + 1, following)

        @block.tensor
        def _(pe):
            def parts3(psum, stat, mov, start, stop):
                for k, (a, b) in enumerate(((0, 0), (0, 1), (1, 0))):
                    last = nc.tensor.matmul(psum, stat(a), mov(b), start=start and k == 0, stop=stop and k == 2,
                                            skip_group_check=True)
                return last

            pe.wait_ge(const_full, 16)
            pe.wait_ge(wsmall_full, 32)
            for c in range(NC):
                last = nc.tensor.transpose(ps[:, 4, c * XP:(c + 1) * XP], wx_nat[:, c * P:(c + 1) * P],
                                           ident[0:XP, 0:XP])
            for c in range(NC):
                last = nc.tensor.transpose(ps[0:R, 5 + c // 4, c % 4 * P:(c % 4 + 1) * P], wdt_nat[:, c, :], ident)
            last.then_inc(small_t, 1)
            for n in range(UNITS):
                kind, k = KIND[n]
                if n in (0, NC):
                    pe.wait_ge(win_full, 16 * (n // NC + 1))
                if n == 2 * NC:
                    pe.wait_ge(wout_full, 16)
                if n == DEQ:
                    pe.wait_ge(scale_split, 1)
                    pe.wait_ge(small_copied, 1)
                if n == DEQ + 2 * NF:
                    pe.wait_ge(dscale_split, 1)
                if n >= 4:
                    pe.wait_ge(prep_lo, n - 3)
                w = width(k) if kind in ("g", "up", "down") else P
                for f in range(KT):
                    bank = ps[:, n % 4, f * P:(f + 1) * P]
                    if kind in ("u", "gate"):
                        last = nc.tensor.transpose(bank, win_tiles[n // NC][:, n % NC, f * P:(f + 1) * P], ident)
                    elif kind == "wout":
                        last = nc.tensor.transpose(bank, wout_nat[:, f, k * P:(k + 1) * P], ident)
                    elif kind in ("g", "up"):
                        col = (kind == "up") * F + k * P
                        rows = pick[:, f * P:(f + 1) * P]
                        nc.tensor.matmul(ps[:, n % 4, f * P:f * P + w], rows, sc_parts[:, col:col + w],
                                         start=True, stop=True)
                        last = nc.tensor.matmul(ps[:, 4 + n % 4, f * P:f * P + w], rows, z_rows[:, col:col + w],
                                                start=True, stop=True)
                if kind == "down":
                    rows = dpick[:, k * P:k * P + w]
                    nc.tensor.matmul(ps[0:w, n % 4, :], rows, dsc_parts, start=True, stop=True)
                    last = nc.tensor.matmul(ps[0:w, 4 + n % 4, :], rows, dz_rows, start=True, stop=True)
                last.then_inc(prep_mm, 1)
            pe.wait_ge(prep_lo, UNITS)
            pe.sem_inc(nsum_done, STEPS)

            def project(i, kind, bank, w):
                ring = ring_b if kind[0] in ("g", "up") else ring_a
                if ring is ring_a:
                    slot, _ = a_use(i, kind)
                    pe.wait_ge(a_full[slot], 16 * fill_count(i, kind))
                else:
                    n = RING_B.index(kind)
                    slot = n % NBR
                    pe.wait_ge(b_full[slot], 16 * (len(RING_B) // NBR * i + (n // NBR + 1)))
                psum_free(pe, i, kind)
                for f in range(KT):
                    last = parts3(PB[bank][0:w, :], lambda a: ring[:, slot, a, f * P:f * P + w],
                                  lambda b: xT[:, b, f, :], f == 0, f == KT - 1)
                last.then_inc(p_full, 1)

            def into_acc(ring, slot, rows, hl, last_of_block, done):
                for t in range(KT):
                    last = parts3(acc[:, t, :], lambda a: hl[0:rows, a, t * P:(t + 1) * P],
                                  lambda b: ring[0:rows, slot, b, :], False, last_of_block)
                last.then_inc(done, 1)

            def transposes(i, t):
                kind = ("xt", t)
                bank, _, _ = psum_use(i, kind)
                psum_free(pe, i, kind)
                for f in range(KT):
                    last = nc.tensor.transpose(PB[bank][:, f * P:(f + 1) * P], lnx[t][:, f * P:(f + 1) * P], ident)
                last.then_inc(p_full, 1)

            def x_project(m, c):
                if c == 0:
                    pe.wait_ge(xdn_ready, m)
                pe.wait_ge(u_ready, NC * m + (c + 1))
                last = nc.tensor.matmul(M[0:XP, :], WxT[:, c, :], u[:, c, :], start=(c == 0), stop=(c == NC - 1),
                                        skip_group_check=True)
                if c == NC - 1:
                    last.then_inc(wx_done, 1)

            def mean_squares(i, m):
                bank, _, _ = psum_use(i, ("ms", 0))
                psum_free(pe, i, ("ms", 0))
                pe.wait_ge(sq_ready, m + 1)
                nc.tensor.matmul(PB[bank], mean_m[0:XP, :], sp_z[0:XP, 0, :], start=True, stop=True,
                                 skip_group_check=True).then_inc(p_full, 1)

            def delta_rows(i, c, m):
                bank, _, _ = psum_use(i, ("dtz", c))
                psum_free(pe, i, ("dtz", c))
                if m is not None:
                    pe.wait_ge(xdn_ready, m + 1)
                nc.tensor.matmul(PB[bank], WdtT[:, c * P:(c + 1) * P], xdn[:], start=True, stop=True,
                                 skip_group_check=True).then_inc(p_full, 1)

            for t in range(KT):
                if t == 0:
                    pe.wait_ge(ln_norm, 1)
                transposes(None, t)
            pe.wait_ge(xt_ready, KT)
            for c in range(NC):
                bank, _, _ = psum_use(None, ("u", c))
                project(None, ("u", c), bank, P)
            for c in range(NC):
                x_project(0, c)
            mean_squares(None, 0)
            delta_rows(None, 0, 0)
            delta_rows(None, 1, 0)

            def state_sum(i, s):
                c, g = divmod(s, SPC)
                pe.wait_ge(p_done, step_no(i, s))
                if g == 0:
                    pe.wait_ge(y_added, NC * i + c)
                for k in range(PAIR):
                    last = nc.tensor.matmul(Y, ident, hb[:, s % NHB, k, :], start=(g == 0 and k == 0),
                                            stop=(g == SPC - 1 and k == PAIR - 1), skip_group_check=True)
                last.then_inc(nsum_done, 1)

            with pe.Fori(0, BLOCKS) as i:
                for s in range(STEPS + 2):
                    if s >= 2:
                        state_sum(i, s - 2)
                    if s > STEPS:
                        continue
                    for j in at(FFN_STEP, s):
                        for kind in (("g", j), ("up", j)):
                            bank, _, _ = psum_use(i, kind)
                            project(i, kind, bank, width(j))
                    for c in at(GATE_STEP, s):
                        bank, _, _ = psum_use(i, ("gate", c))
                        project(i, ("gate", c), bank, P)
                    for q in at(DTZ_STEP, s):
                        delta_rows(i, 2 * q + 2, None)
                        delta_rows(i, 2 * q + 3, None)
                    for t in at(RES_STEP, s):
                        if t == 0:
                            pe.wait_ge(out_evac, KT * i)
                        pe.wait_ge(tok_full[t % 2], 16 * (2 * i + (t // 2 + 1)))
                        nc.tensor.matmul(acc[:, t, :], ident, tok[:, t % 2, :], start=True, stop=False,
                                         skip_group_check=True).then_inc(res_done, 1)
                    for j in at(DOWN_STEP, s):
                        n = RING_B.index(("down", j))
                        pe.wait_ge(b_full[n % NBR], 16 * (len(RING_B) // NBR * i + (n // NBR + 1)))
                        pe.wait_ge(hl_ready, NF * i + (j + 1))
                        into_acc(ring_b, n % NBR, width(j), h_hl, False, down_done)
                    for t in at(XT_STEP, s):
                        if t == 0:
                            pe.wait_ge(ln_norm, i + 2)
                        transposes(i, t)
                    for c in at(U_STEP, s):
                        if c == 0:
                            pe.wait_ge(xt_ready, KT * (i + 2))
                        bank, _, _ = psum_use(i, ("u", c))
                        project(i, ("u", c), bank, P)
                    for c in at(WX_STEP, s):
                        x_project(i + 1, c)
                    if s == MS_STEP:
                        mean_squares(i, i + 1)
                    for c in at(WOUT_STEP, s):
                        if c < NC - 1:
                            out_project(pe, into_acc, i, c)
                delta_rows(i, 0, i + 1)
                delta_rows(i, 1, i + 1)
                out_project(pe, into_acc, i, NC - 1)


        @block.scalar
        def _(act):
            links = [0, 0, 0]

            def link(ins, i):
                links[i is not None] += 1
                ins.then_inc(act_link, 1)
                n = links[i is not None]
                act.wait_ge(act_link, n if i is None else ACT_LINKS * i + (links[0] + n))

            act.wait_ge(small_t, 1)
            act.wait_ge(zeroed, ZEROED)
            nc.scalar.copy(WxT[:].rearrange("p c m -> p (c m)"), ps[:, 4, :])
            nc.scalar.copy(WdtT[0:R, :].rearrange("p (h d) -> p h d", h=2), ps[0:R, 5:7, :]).then_inc(small_copied, 1)
            for n in range(UNITS):
                if n < DEQ:
                    act.wait_ge(prep_mm, n + 1)
                    src = ps[:, n % 4, :].rearrange("p (a t) -> p a t", a=1)
                else:
                    act.wait_ge(prep_w, n - DEQ + 1)
                    src = conv[:, n % 2, :].rearrange("p (a t) -> p a t", a=1)
                if n >= 2:
                    act.wait_ge(stored[n % 2], 16 * (n // 2))
                nc.scalar.copy(unit_view(stage[n % 2][:, 0:1, :], n), unit_view(src, n)).then_inc(prep_hi, 1)
            act.sem_inc(exp_done, STEPS)

            def layer_norm(m):
                act.wait_ge(ln_stats, m + 1)
                for t in range(KT):
                    last = nc.scalar.activation(lnx[t][:], lnx[t][:], ACT.Identity, bias=nmr[:, t:t + 1],
                                                scale=rstd[:, t:t + 1])
                last.then_inc(ln_norm, 1)

            def x_high(i, t):
                bank, full, _ = psum_use(i, ("xt", t))
                act.wait_ge(p_full, full)
                nc.scalar.copy(xT[:, 0, :, t * P:(t + 1) * P],
                               PB[bank].rearrange("p (k t) -> p k t", k=KT)).then_inc(xh_ready, 1)

            def u_evacuate(i, m, c):
                bank, full, _ = psum_use(i, ("u", c))
                act.wait_ge(p_full, full)
                if m is not FIRST or c >= NCV:
                    act.wait_ge(u_ready, NC * m + (c - NCV + 1))
                nc.scalar.copy(u_raw[:, c % NCV, HALO:], PB[bank])
                nc.scalar.activation(conv[:, c % NCV, :], PB[bank], ACT.Identity, bias=cb[:, c:c + 1],
                                     scale=cw[:, c, TAPS - 1:TAPS]).then_inc(p_read[bank], 1)

            def u_tanh(m, c):
                act.wait_ge(cv_ready, NC * m + (c + 1))
                if m is not FIRST or c >= 1:
                    act.wait_ge(u_ready, NC * m + c)
                nc.scalar.activation(e_cg[:], conv[:, c % NCV, :], ACT.Tanh).then_inc(ue_ready, 1)

            def squares(m):
                act.wait_ge(wx_done, m + 1)
                if m is not FIRST:
                    act.wait_ge(delta_ready, NC // 2 * m)
                nc.scalar.activation(sp_z[0:XP, 0, :], M[0:XP, :], ACT.Square).then_inc(sq_ready, 1)

            def store_bc(m):
                act.wait_ge(xdn_ready, m + 1)
                act.dma_start(bc_dram, xdn[R:XP, :]).then_inc(bc_stored, 16)

            def softplus(i, q, pairs):
                if i is not None:
                    act.wait_ge(delta_ready, pairs)
                for c in (2 * q, 2 * q + 1):
                    bank, full, read = psum_use(i, ("dtz", c))
                    act.wait_ge(p_full, full)
                    nc.scalar.activation(sp_z[:, c % 2, :], PB[bank], ACT.Identity, bias=dtb[:, c:c + 1])
                    nc.scalar.activation(sp_l[:, c % 2, :], PB[bank], ACT.Abs,
                                         bias=dtb[:, c:c + 1]).then_inc(p_read[bank], 1)
                for c in (2 * q, 2 * q + 1):
                    bank, _, read = psum_use(i, ("dtz", c))
                    act.wait_ge(p_read[bank], read)
                link(nc.scalar.activation(sp_l[:], sp_l[:], ACT.Exp, scale=-1.0), i)
                nc.scalar.activation(sp_l[:], sp_l[:], ACT.Ln, bias=1.0).then_inc(sp_ready, 1)

            layer_norm(FIRST)
            for t in range(KT):
                x_high(None, t)
            for c in range(NC + 1):
                if c < NC:
                    u_evacuate(None, FIRST, c)
                if c >= 1:
                    u_tanh(FIRST, c - 1)
            squares(FIRST)
            store_bc(FIRST)
            softplus(None, 0, 0)

            def broadcast(i, rows, tile, g, full):
                act.dma_start(tile[:, g * PAIR:(g + 1) * PAIR, :],
                              bc_dram[rows + g * PAIR:rows + (g + 1) * PAIR, :].partition_broadcast(P)
                              ).then_inc(full[g], 16)

            def b_rows(i, g):
                act.wait_ge(dbu_done, step_no(i, g - SPC))
                broadcast(i, 0, B_bc, g, bb_full)

            with act.Fori(0, BLOCKS) as i:
                for s in range(STEPS):
                    c, g = divmod(s, SPC)
                    if s == 0:
                        act.wait_ge(bc_stored, 16 * (i + 1))
                        b_rows(i, 0)
                        b_rows(i, 1)
                    if s + 2 < SPC:
                        b_rows(i, s + 2)
                    if s < SPC:
                        act.wait_ge(p_done, step_no(i, s - SPC))
                        broadcast(i, N, C_bc, s, cb_full)
                    if g == 0:
                        act.wait_ge(delta_ready, NC // 2 * i + (c // 2 + 1))
                    act.wait_ge(scan_done, step_no(i, s - NDA))
                    for k in range(PAIR):
                        last = nc.scalar.activation(dA[:, s % NDA, k, :], delta[:, c % 4, :], ACT.Exp,
                                                    scale=A_sb[:, c, g * PAIR + k:g * PAIR + k + 1])
                    last.then_inc(exp_done, 1)
                    if g == 5:
                        act.wait_ge(yl_ready, NC * i + c)
                        act.wait_ge(u_ready, NC * i + (c + 1))
                        nc.scalar.activation(ud[:], u[:, c, :], ACT.Copy,
                                             scale=dpar[:, c:c + 1]).then_inc(ud_ready, 1)
                    for j in at(FFN_STEP, s - 1):
                        w = width(j)
                        bank, full, _ = psum_use(i, ("g", j))
                        act.wait_ge(p_full, full)
                        act.wait_ge(hl_ready, NF * i + j)
                        nc.scalar.activation(ffn_e[0:w, :], PB[bank][0:w, :], ACT.Tanh, scale=0.5)
                        nc.scalar.mul(ffn_g[0:w, :], PB[bank][0:w, :], 0.5).then_inc(p_read[bank], 1)
                        bank, full, _ = psum_use(i, ("up", j))
                        act.wait_ge(p_full, full)
                        nc.scalar.copy(ffn_u[0:w, :], PB[bank][0:w, :]).then_inc(p_read[bank], 1)
                    for j in at(FFN_STEP, s - 2):
                        w = width(j)
                        act.wait_ge(h_ready, NF * i + (j + 1))
                        act.wait_ge(down_done, NF * i + j)
                        nc.scalar.copy(h_hl[0:w, 0, :], ffn_u[0:w, :]).then_inc(hh_ready, 1)
                    for cc in at(GATE_STEP, s - 1):
                        bank, full, _ = psum_use(i, ("gate", cc))
                        act.wait_ge(p_full, full)
                        act.wait_ge(gate_ready, NC * i + cc)
                        act.wait_ge(y_gated, NC * i + max(cc - NGATE + 1, 0))
                        nc.scalar.activation(gate_e[:], PB[bank], ACT.Tanh, scale=0.5)
                        nc.scalar.mul(gate[:, cc % NGATE, :], PB[bank], 0.5).then_inc(p_read[bank], 1)
                    for q in at(DTZ_STEP, s - 1):
                        softplus(i, q + 1, NC // 2 * i + (q + 1))
                    for cc in at(WOUT_STEP, s + 1):
                        if cc < NC - 1:
                            y_high(i, cc)
                    if s == XT_STEP[0] - 2:
                        layer_norm(i + 1)
                    for t in at(XT_STEP, s - 1):
                        x_high(i, t)
                    for cc in at(U_STEP, s - 1):
                        u_evacuate(i, i + 1, cc)
                    for cc in at(U_STEP, s - 3):
                        u_tanh(i + 1, cc)
                    if s == MS_STEP:
                        squares(i + 1)
                store_bc(i + 1)
                softplus(i, 0, NC // 2 * (i + 1))
                y_high(i, NC - 1)
                act.wait_ge(wout_done, NC * (i + 1))
                for t in range(KT):
                    if t >= 2:
                        act.wait_ge(tok_out[t % 2], 16 * (2 * i + 1))
                    nc.scalar.copy(tok[:, t % 2, :], acc[:, t, :]).then_inc(out_evac, 1)
                    act.wait_ge(out_evac, KT * i + (t + 1))
                    act.dma_start(out_tok[i, t], tok[:, t % 2, :]).then_inc(tok_out[t % 2], 16)
            act.wait_ge(tok_out[0], 32 * BLOCKS)
            act.wait_ge(tok_out[1], 32 * BLOCKS)
            act.wait_ge(bc_stored, 16 * (BLOCKS + 1))
            assert links[1] == ACT_LINKS, links

        @block.gpsimd
        def _(pool):
            for tile in (sc_parts, z_rows, pick, dsc_parts, dz_rows, dpick, WdtT[:], xdn[:], carry[:], halo[:]):
                nc.gpsimd.memset(tile.bitcast(F32), 0.0).then_inc(zeroed, 1)
            pool.sem_inc(dbu_done, STEPS)

            def rsqrt_var(m):
                pool.wait_ge(ln_var, m + 1)
                nc.gpsimd.tensor_tensor(rstd[:], rstd[:], minus_half.broadcast_to([P, KT]),
                                        ALU.pow).then_inc(ln_pow, 1)

            def rsqrt_mean(i, m):
                bank, _, read = psum_use(i, ("ms", 0))
                pool.wait_ge(p_read[bank], read)
                nc.gpsimd.tensor_tensor(sp_l[0:XP, 0, :], sp_l[0:XP, 0, :],
                                        minus_half[0:XP, :].broadcast_to([XP, T]),
                                        ALU.pow).then_inc(ms_pow, 1)

            rsqrt_var(FIRST)
            rsqrt_mean(None, FIRST)
            with pool.Fori(0, BLOCKS) as i:
                for s in range(STEPS):
                    c, g = divmod(s, SPC)
                    if g == 0:
                        pool.wait_ge(du_ready, NC * i + (c + 1))
                    if c == 0:
                        pool.wait_ge(bb_full[g], 16 * (i + 1))
                    pool.wait_ge(nsum_done, step_no(i, s - NHB))
                    nc.gpsimd.tensor_tensor(hb[:, s % NHB, :, :], B_bc[:, g * PAIR:(g + 1) * PAIR, :],
                                            du[:, c % 2, :].unsqueeze(1).broadcast_to([P, PAIR, T]),
                                            ALU.mult).then_inc(dbu_done, 1)
                    for j in at(FFN_STEP, s - 3):
                        w = width(j)
                        pool.wait_ge(hh_ready, NF * i + (j + 1))
                        nc.gpsimd.tensor_tensor(h_hl[0:w, 1, :], ffn_u[0:w, :], h_hl[0:w, 0, :].bitcast(F32),
                                                ALU.subtract).then_inc(hl_ready, 1)
                    for cc in at(WOUT_STEP, s + 1):
                        if cc < NC - 1:
                            y_low(i, cc)
                    if s == XT_STEP[0] - 3:
                        rsqrt_var(i + 1)
                rsqrt_mean(i, i + 1)
                y_low(i, NC - 1)

        @block.vector
        def _(dve):
            links = [0, 0]

            def link(ins, i=None):
                links[i is not None] += 1
                ins.then_inc(vec_link, 1)
                n = links[i is not None]
                dve.wait_ge(vec_link, n if i is None else VEC_LINKS * i + (links[0] + n))

            def group_rows(idx, groups, tmp, pick_rows, n, parts):
                link(nc.vector.tensor_scalar(tmp, idx.bitcast(I32), 0.0, float(groups), ALU.is_lt, ALU.mult))
                link(nc.vector.tensor_tensor(tmp, tmp, idx.bitcast(I32), ALU.add))
                link(nc.vector.tensor_scalar(tmp, tmp, 0.0, float(groups - 1), ALU.max, ALU.min))
                for lo in range(parts):
                    link(nc.vector.tensor_scalar(pick_rows[LOW * lo:LOW * lo + groups, :], tmp,
                                                 row_col[0:groups, :], None, ALU.is_equal))

            def scale_rows(raw, zero_words, zeros, groups, parts, rows):
                zv = zeros.rearrange("g (w k) -> g w k", k=8)
                for k in range(8):
                    last = nc.vector.tensor_scalar(zv[:, :, k], zero_words, 4 * k, 15, ALU.logical_shift_right,
                                                   ALU.bitwise_and)
                link(last)
                nc.vector.tensor_scalar(rows[0:groups, :], zeros, 1.0, None, ALU.add)
                link(nc.vector.tensor_copy(parts[0:groups, :], raw))
                nc.vector.tensor_tensor(parts[LOW:LOW + groups, :], raw, parts[0:groups, :].bitcast(F32),
                                        ALU.subtract)

            dve.wait_ge(const_full, 16 * 9)
            link(nc.vector.tensor_copy(shift[:], row_col))
            link(nc.vector.tensor_scalar(shift[:], shift[:], 7, 2, ALU.bitwise_and, ALU.logical_shift_left))
            dve.wait_ge(zeroed, ZEROED)
            nc.vector.tensor_scalar(cw[:], cw[:], 0.5, None, ALU.mult)
            link(nc.vector.tensor_scalar(cb[:], cb[:], 0.5, None, ALU.mult))

            def low_part(n):
                src = ps[:, n % 4, :] if n < DEQ else conv[:, n % 2, :]
                dve.wait_ge(prep_hi, n + 1)
                nc.vector.tensor_tensor(unit_view(stage[n % 2][:, 1:2, :], n),
                                        unit_view(src.rearrange("p (a t) -> p a t", a=1), n),
                                        unit_view(stage[n % 2][:, 0:1, :], n).bitcast(F32),
                                        ALU.subtract).then_inc(prep_lo, 1)

            for n in range(NC):
                low_part(n)
            dve.wait_ge(scale_full, 48)
            dve.wait_ge(dscale_full, 32)
            group_rows(gidx, G_GU, ffn_g[0:G_GU, :], pick, HID, 2)
            scale_rows(sc_raw, qz_raw, z_int, G_GU, sc_parts, z_rows)
            nc.vector.memset(st6[:], 0.0).then_inc(scale_split, 1)
            for n in range(NC, DEQ):
                low_part(n)
            for n in range(DEQ, UNITS):
                kind, k = KIND[n]
                w = width(k)
                d = n - DEQ
                if kind == "down" and k == 0:
                    dve.wait_ge(prep_lo, n)
                if kind == "down":
                    dve.wait_ge(dwords_full[k % 4], 16 * 8 * (k // 4 + 1))
                    src = dwords[0:w, k % 4, :]
                    wi = w_int[n % 2][0:w, :].bitcast(U32)
                    Z, S, W = ps[0:w, 4 + n % 4, :], ps[0:w, n % 4, :], conv[0:w, n % 2, :]
                else:
                    if d == 0:
                        dve.wait_ge(words_full, 128)
                    col = (kind == "up") * F + k * P
                    src = words[:, :, col:col + w]
                    wi, Z, S, W = (t.rearrange("p (k f) -> p k f", k=KT)[:, :, 0:w] for t in
                                   (w_int[n % 2].bitcast(U32), ps[:, 4 + n % 4, :], ps[:, n % 4, :],
                                    conv[:, n % 2, :]))
                rows = w if kind == "down" else P
                link(nc.vector.tensor_scalar(wi, src, shift[0:rows, :], 15, ALU.logical_shift_right,
                                             ALU.bitwise_and))
                dve.wait_ge(prep_mm, n + 1)
                link(nc.vector.tensor_tensor(wi.bitcast(F32), wi, Z, ALU.subtract))
                nc.vector.tensor_tensor(W, wi.bitcast(F32), S, ALU.mult).then_inc(prep_w, 1)
                low_part(n)
                if n == DEQ + 4:
                    dve.wait_ge(dscale_full, 48)
                    group_rows(didx, G_D, gate[0:G_D, :, :].rearrange("p a t -> p (a t)")[:, 0:F], dpick, F, 2)
                    scale_rows(dsc_raw, dqz_raw, dz_int, G_D, dsc_parts, dz_rows)
                    nc.vector.memset(st6[:], 0.0).then_inc(dscale_split, 1)
            dve.sem_inc(scan_done, STEPS)
            dve.sem_inc(p_done, STEPS)

            def ln_statistics(i, m):
                dve.wait_ge(ln_full, 16 * KT * (m + 1))
                for t in range(KT):
                    last = nc.vector.bn_stats(st6[:, t, :], lnx[t][:])
                link(last, i)
                nc.vector.memset(rstd[:], 0.0)
                for t in range(KT):
                    last = nc.vector.bn_aggr(mv[:, t, :], st6[:, t, :])
                link(last, i)
                nc.vector.tensor_scalar(rstd[:], mv[:, :, 1], EPS_LN, None, ALU.add).then_inc(ln_var, 1)
                dve.wait_ge(ln_pow, m + 1)
                nc.vector.scalar_tensor_tensor(nmr[:], mv[:, :, 0], -1.0, rstd[:], ALU.mult,
                                               ALU.mult).then_inc(ln_stats, 1)

            def x_low(i, t):
                bank, _, _ = psum_use(i, ("xt", t))
                m_count = (t + 1) if i is None else KT * (i + 1) + (t + 1)
                dve.wait_ge(xh_ready, m_count)
                nc.vector.tensor_tensor(xT[:, 1, :, t * P:(t + 1) * P],
                                        PB[bank].rearrange("p (k t) -> p k t", k=KT),
                                        xT[:, 0, :, t * P:(t + 1) * P].bitcast(F32), ALU.subtract
                                        ).then_inc(p_read[bank], 1)
                if t == KT - 1:
                    for b in range(2):
                        _, _, read = psum_use(i, ("xt", KT - 2 + b))
                        dve.wait_ge(p_read[psum_use(i, ("xt", KT - 2 + b))[0]], read)
                    dve.sem_inc(xt_ready, KT)

            def taps(i, m, c):
                bank, _, read = psum_use(i, ("u", c))
                dve.wait_ge(p_read[bank], read)
                link(nc.vector.tensor_scalar(u_raw[:, c % NCV, 0:HALO], halo[:, c, :],
                                             cst[:, bass.ds(m + lim0, 1)], cst[:, bass.ds(m + (lim0 + nlim), 1)],
                                             ALU.min, ALU.max), i)
                nc.vector.tensor_copy(halo[:, c, :], u_raw[:, c % NCV, T:T + HALO])
                for k in range(TAPS - 1):
                    ins = nc.vector.scalar_tensor_tensor(conv[:, c % NCV, :], u_raw[:, c % NCV, k:k + T],
                                                         cw[:, c, k:k + 1], conv[:, c % NCV, :], ALU.mult, ALU.add)
                    if k < TAPS - 2:
                        link(ins, i)
                ins.then_inc(cv_ready, 1)

            def u_silu(i, m, c):
                dve.wait_ge(ue_ready, NC * m + (c + 1))
                if m is not FIRST:
                    dve.wait_ge(ud_ready, NC * m + (c + 1 - NC))
                nc.vector.scalar_tensor_tensor(u[:, c, :], e_cg[:], 1.0, conv[:, c % NCV, :], ALU.add,
                                               ALU.mult).then_inc(u_ready, 1)

            def mean_rows(i, m):
                bank, full, read = psum_use(i, ("ms", 0))
                dve.wait_ge(p_full, full)
                nc.vector.tensor_scalar(sp_l[0:XP, 0, :], PB[bank][0:XP, :], EPS_RMS, None,
                                        ALU.add).then_inc(p_read[bank], 1)

            def norm_rows(m):
                dve.wait_ge(ms_pow, m + 1)
                if m is not FIRST:
                    dve.wait_ge(bc_stored, 16 * m)
                nc.vector.scalar_tensor_tensor(xdn[0:XP, :], M[0:XP, :], lnw[0:XP, 0:1], sp_l[0:XP, 0, :],
                                               ALU.mult, ALU.mult).then_inc(xdn_ready, 1)

            def delta_pair(pairs, q=0):
                dve.wait_ge(sp_ready, pairs + 1)
                if pairs is not FIRST:
                    dve.wait_ge(exp_done, 2 * SPC * pairs + (STEPS - 2 * SPC))
                nc.vector.scalar_tensor_tensor(delta[:, q % 2 * 2:q % 2 * 2 + 2, :], sp_z[:], 0.0, sp_l[:], ALU.max,
                                               ALU.add).then_inc(delta_ready, 1)

            def du_rows(c, chunks, pairs):
                if chunks is not FIRST:
                    dve.wait_ge(dbu_done, SPC * chunks + (STEPS - SPC))
                dve.wait_ge(delta_ready, pairs + 1)
                dve.wait_ge(u_ready, chunks + 1)
                nc.vector.tensor_tensor(du[:, c % 2, :], delta[:, c % 4, :], u[:, c, :],
                                        ALU.mult).then_inc(du_ready, 1)

            ln_statistics(None, FIRST)
            for t in range(KT):
                x_low(None, t)
            for c in range(NC + 1):
                if c < NC:
                    taps(None, FIRST, c)
                if c >= 1:
                    u_silu(None, FIRST, c - 1)
            mean_rows(None, FIRST)
            norm_rows(FIRST)
            delta_pair(FIRST)
            du_rows(0, FIRST, FIRST)

            def keep_state(i, s):
                c, g = divmod(s, SPC)
                dve.wait_ge(scan_done, step_no(i, s))
                n = c * N + g * PAIR
                return nc.vector.tensor_copy(carry[:, n:n + PAIR], hb[:, s % NHB, :, T - 1])

            def times_c(i, s):
                c, g = divmod(s, SPC)
                if c == 0:
                    dve.wait_ge(cb_full[g], 16 * (i + 1))
                nc.vector.tensor_tensor(hb[:, s % NHB, :, :], hb[:, s % NHB, :, :],
                                        C_bc[:, g * PAIR:(g + 1) * PAIR, :], ALU.mult).then_inc(p_done, 1)

            def gated_y(i, c):
                dve.wait_ge(nsum_done, step_no(i, SPC * (c + 1) - 1))
                dve.wait_ge(ud_ready, NC * i + (c + 1))
                dve.wait_ge(gate_ready, NC * i + (c + 1))
                nc.vector.tensor_tensor(ud[:], Y, ud[:], ALU.add).then_inc(y_added, 1)
                dve.wait_ge(y_added, NC * i + (c + 1))
                nc.vector.tensor_tensor(ud[:], ud[:], gate[:, c % NGATE, :], ALU.mult).then_inc(y_gated, 1)

            with dve.Fori(0, BLOCKS) as i:
                links[1] = 0
                link(nc.vector.tensor_scalar(carry[:], carry[:], cst[:, bass.ds(i + lim0, 1)],
                                             cst[:, bass.ds(i + (lim0 + nlim), 1)], ALU.min, ALU.max), i)
                for s in range(STEPS):
                    c, g = divmod(s, SPC)
                    if s >= SPC + 2 and g == 2:
                        gated_y(i, c - 1)
                    dve.wait_ge(exp_done, step_no(i, s))
                    dve.wait_ge(dbu_done, step_no(i, s))
                    for k in range(PAIR):
                        if k == 1 and s >= 1:
                            kept = keep_state(i, s - 1)
                            kept.then_inc(vec_link, 1)
                            links[1] += 1
                            mark = links[1]
                        n = c * N + g * PAIR + k
                        last = nc.vector.tensor_tensor_scan(hb[:, s % NHB, k, :], dA[:, s % NDA, k, :],
                                                            hb[:, s % NHB, k, :], carry[:, n:n + 1],
                                                            ALU.mult, ALU.add)
                    last.then_inc(scan_done, 1)
                    if s >= 1:
                        dve.wait_ge(vec_link, VEC_LINKS * i + (links[0] + mark))
                        times_c(i, s - 1)
                    for j in at(FFN_STEP, s - 1):
                        w = width(j)
                        for kind in (("g", j), ("up", j)):
                            bank, _, read = psum_use(i, kind)
                            dve.wait_ge(p_read[bank], read)
                        link(nc.vector.scalar_tensor_tensor(ffn_g[0:w, :], ffn_e[0:w, :], 1.0, ffn_g[0:w, :],
                                                            ALU.add, ALU.mult), i)
                        nc.vector.tensor_tensor(ffn_u[0:w, :], ffn_g[0:w, :], ffn_u[0:w, :],
                                                ALU.mult).then_inc(h_ready, 1)
                    for cc in at(GATE_STEP, s - 1):
                        bank, _, read = psum_use(i, ("gate", cc))
                        dve.wait_ge(p_read[bank], read)
                        nc.vector.scalar_tensor_tensor(gate[:, cc % NGATE, :], gate_e[:], 1.0,
                                                       gate[:, cc % NGATE, :], ALU.add,
                                                       ALU.mult).then_inc(gate_ready, 1)
                    for q in at(DTZ_STEP, s - 2):
                        delta_pair(NC // 2 * i + (q + 1), q + 1)
                    if g == 5 and c < NC - 1:
                        du_rows(c + 1, NC * i + (c + 1), NC // 2 * i + (c + 1) // 2)
                    if s == XT_STEP[0] - 3:
                        ln_statistics(i, i + 1)
                    for t in at(XT_STEP, s - 1):
                        x_low(i, t)
                    for cc in at(U_STEP, s - 2):
                        taps(i, i + 1, cc)
                    for cc in at(U_STEP, s - 4):
                        u_silu(i, i + 1, cc)
                    if s == STEPS - 1:
                        mean_rows(i, i + 1)
                link(keep_state(i, STEPS - 1), i)
                times_c(i, STEPS - 1)
                norm_rows(i + 1)
                delta_pair(NC // 2 * (i + 1))
                du_rows(0, NC * (i + 1), NC // 2 * (i + 1))
                gated_y(i, NC - 1)
            assert links[1] == VEC_LINKS, links


_INS = ["L0_attn_hidden_states", "L0_attn_W_in", "L0_attn_conv_w", "L0_attn_conv_b", "L0_attn_Wx",
        "L0_attn_dt_ln_w", "L0_attn_b_ln_w", "L0_attn_c_ln_w", "L0_attn_Wdt", "L0_attn_dt_bias", "L0_attn_A",
        "L0_attn_D_param", "L0_attn_W_out", "L0_ffn_qweight_gu", "L0_ffn_qzeros_gu", "L0_ffn_scales_gu",
        "L0_ffn_g_idx_gu", "L0_ffn_qweight_down", "L0_ffn_qzeros_down", "L0_ffn_scales_down",
        "L0_ffn_g_idx_down"]


def constants(batch, length):
    import numpy as np

    per = length // T
    blocks = batch * per
    mean = np.zeros((P, P), np.float32)
    for lo, hi in ((0, R), (R, R + N), (R + N, XP)):
        mean[lo:hi, lo:hi] = 1.0 / (hi - lo)
    limits = [0.0 if m % per == 0 else 3.0e38 for m in range(blocks + 1)]
    cols = [np.eye(P, dtype=np.float32), mean, np.arange(P, dtype=np.float32)[:, None],
            np.full((P, 1), -0.5, np.float32)]
    cols += [np.tile(np.array([v], np.float32), (P, 1)) for v in limits + [-v for v in limits]]
    return np.concatenate(cols, axis=1)


def kernel(**inputs):
    import concourse.bacc as bacc
    import numpy as np
    from concourse.bass_utils import run_bass_kernel_spmd

    nc = bacc.Bacc("TRN2", target_bir_lowering=False, num_devices=1, dynamic_dma_scratch_size=1024)
    arrays, args = {}, []
    for name in _INS:
        a = np.ascontiguousarray(inputs[name])
        arrays[name] = a
        args.append(nc.dram_tensor(name, a.shape, mybir.dt.from_np(a.dtype), kind="ExternalInput").ap())
    shape = arrays[_INS[0]].shape
    arrays["consts"] = constants(shape[0], shape[1])
    args.append(nc.dram_tensor("consts", arrays["consts"].shape, F32, kind="ExternalInput").ap())
    args.append(nc.dram_tensor("out", shape, F32, kind="ExternalOutput").ap())
    build(nc, *args)
    r = run_bass_kernel_spmd(nc, [arrays], core_ids=[0])
    return r.results[0]["out"]
```

```python
from contextlib import ExitStack

import concourse.bass as bass
from concourse import mybir

ALU = mybir.AluOpType
ACT = mybir.ActivationFunctionType
F32 = mybir.dt.float32
F32R = mybir.dt.float32r
U32 = mybir.dt.uint32
I32 = mybir.dt.int32

P = 128
T = 512
HID = 512
KT = HID // P
D = 1024
NC = D // P
N = 16
R = 32
XP = R + 2 * N
TAPS = 4
HALO = TAPS - 1
F = 1376
NF = -(-F // P)
GROUP = 128
G_GU = HID // GROUP
G_D = F // GROUP
EPS_LN = 1e-5
EPS_RMS = 1e-6

PAIR = 2
SPC = N // PAIR
STEPS = NC * SPC
FIRST = 0

NA, NBR = 3, 3
NDA, NHB = 6, 3
NGATE = 4
NCV = 3

HEAD = 8
EXP_LEAD = 1
POOL_LAG = 3
SUM_LAG = 3

G_STEP = [-6, 0, 10, 13, 16, 18, 22, 26, 29, 33, 36]
UP_STEP = [s + 1 for s in G_STEP]
DOWN_STEP = [8, 12, 15, 18, 20, 23, 26, 31, 34, 38, 42]
HIGH_STEP = [-2, 10, 13, 17, 19, 23, 25, 29, 33, 37, 39]
GATE_STEP = [-9, -7, -4, 4, 11, 20, 28, 37]
EARLY = -10
DTZ_STEP = [8, 22, 35]
ROWS_STEP = 60
LOAD_X_STEP = 10
LN_STEP = 22
XT_STEP = [39, 39, 40, 40]
U_STEP = [42, 43, 44, 46, 47, 49, 50, 52]
WX_STEP = [47, 47, 49, 50, 52, 53, 55, 57]
MS_STEP = 57
DTZ0_STEP = 59
WOUT_STEP = [SPC * (c + 1) + 6 for c in range(NC - 1)] + [6]
NOT_PREADDED = {3, 15, 23, 27, 31, 35, 36, 37, 38, 39, 40, 43, 45, 46, 47, 49, 50, 51, 55, 58, 59, 60, 61, 62,
                63}
PREADD = [s not in NOT_PREADDED for s in range(STEPS)]


DA_SLOT = [s % NDA for s in range(STEPS)]
HB_SLOT = [s % NHB for s in range(STEPS - 1)] + [1]


def since(slots, s):
    return next(d for d in range(1, STEPS) if slots[s - d] == slots[s])


def at(steps, s):
    return [n for n, x in enumerate(steps) if x == s]


def width(j):
    return min(P, F - j * P)


def block_items(s):
    return ([("g", j) for j in at(G_STEP, s)] + [("up", j) for j in at(UP_STEP, s)]
            + [("gate", c) for c in at(GATE_STEP, s)])


def items(s):
    order = block_items(s)
    for k in (0, 1):
        order += [("dtz", 2 * q + 2 + k) for q in at(DTZ_STEP, s - k)]
    order += [("down", j) for j in at(DOWN_STEP, s)]
    order += [("xt", t) for t in at(XT_STEP, s)]
    order += [("u", c) for c in at(U_STEP, s)]
    if s == MS_STEP:
        order.append(("ms", 0))
    if s == DTZ0_STEP:
        order += [("dtz", 0), ("dtz", 1)]
    order += [("wout", c) for c in at(WOUT_STEP, s)]
    if s - STEPS >= EARLY:
        order += block_items(s - STEPS)
    return order


ITERATION = [*range(HEAD, STEPS), *range(HEAD)]
ALL_ITEMS = [x for s in ITERATION for x in items(s)]
AHEAD = {x for s in range(EARLY, HEAD) for x in block_items(s)} | {("wout", NC - 1)}
E_ORDER = [x for s in range(EARLY, STEPS) for x in block_items(s) if x[0] != "up"]
PSUM_ORDER = [x for x in ALL_ITEMS if x[0] not in ("down", "wout")]
RING_A = [x for x in ALL_ITEMS if x[0] in ("gate", "u", "wout")]
RING_B = [x for x in ALL_ITEMS if x[0] in ("g", "up", "down")]
PSUM_PRE = PSUM_ORDER.index(("xt", 0))
A_PRE, B_PRE = RING_A.index(("u", 0)), RING_B.index(("g", 0))
FOR_NEXT = {x for x in ALL_ITEMS if x[0] == "u" or x in AHEAD and x[0] != "wout"}
UNIT = {("u", c): c for c in range(NC)}
UNIT |= {("gate", c): NC + c for c in range(NC)}
UNIT |= {("wout", c): 2 * NC + c for c in range(NC)}
UNIT |= {("g", j): 3 * NC + 2 * j for j in range(NF)}
UNIT |= {("up", j): 3 * NC + 2 * j + 1 for j in range(NF)}
UNIT |= {("down", j): 3 * NC + 2 * NF + j for j in range(NF)}
UNITS = len(UNIT)
KIND = {n: kind for kind, n in UNIT.items()}

VEC_LINKS = 110
ACT_LINKS = 12


def build(nc, x, W_in, conv_w, conv_b, Wx, dt_ln_w, b_ln_w, c_ln_w, Wdt, dt_bias, A, D_param, W_out,
          qw_gu, qz_gu, sc_gu, idx_gu, qw_d, qz_d, sc_d, idx_d, consts, out):
    tokens = x.shape[0] * x.shape[1]
    BLOCKS = tokens // T
    LAST = BLOCKS - 1
    assert LAST > 0
    assert len(RING_A) % NA == 0 and len(RING_B) % NBR == 0 and len(set(ALL_ITEMS)) == len(ALL_ITEMS)

    x_tok = x.rearrange("b (k t p) h -> (b k) t p h", p=P, t=T // P)
    out_tok = out.rearrange("b (k t p) h -> (b k) t p h", p=P, t=T // P)

    ctx = ExitStack()
    with ctx:
        def sb(name, shape, dt=F32):
            return ctx.enter_context(nc.sbuf_tensor(name, shape, dt))

        def sem(name):
            return ctx.enter_context(nc.semaphore(name))

        units = nc.dram_tensor("weight_units", [UNITS, P, 2 * T], F32, kind="Internal").ap()
        bc_dram = nc.dram_tensor("bc_rows", [2 * N, T], F32, kind="Internal").ap()

        bc_all = sb("bc_all", [P, 2 * N * T])
        B_bc = bc_all[:, 0:N * T].rearrange("p (n t) -> p n t", n=N)
        C_bc = bc_all[:, N * T:2 * N * T].rearrange("p (n t) -> p n t", n=N)
        ring_a = sb("ring_a", [P, NA, 2, T], F32R)
        ring_b = sb("ring_b", [P, NBR, 2, T], F32R)
        ssm = sb("ssm", [P, (NDA + NHB) * PAIR * T])
        dA = ssm[:, 0:NDA * PAIR * T].rearrange("p (b k t) -> p b k t", b=NDA, k=PAIR)
        hb = ssm[:, NDA * PAIR * T:].rearrange("p (b k t) -> p b k t", b=NHB, k=PAIR)
        xT = sb("xT", [P, 2, KT, T], F32R)
        u = sb("u", [P, NC, T])
        gate = sb("gate", [P, NGATE, T])
        ffn_e = sb("ffn_e", [P, T])
        ffn_g = sb("ffn_g", [P, T])
        ffn_u = sb("ffn_u", [P, T])
        h_hl = sb("h_hl", [P, 2, T], F32R)
        y_hl = sb("y_hl", [P, 2, T], F32R)
        u_raw = sb("u_raw", [P, NCV, T + HALO])
        conv = sb("conv", [P, NCV, T])
        e_cg = sb("e_cg", [P, T])
        sp_l = sb("sp_l", [P, 2, T])
        delta = sb("delta", [P, 4, T])
        du = sb("du", [P, 2, T])
        ud = sb("ud", [P, 2, T])
        xdn = sb("xdn", [P, T])
        WxT = sb("WxT", [P, NC, XP])
        WdtT = sb("WdtT", [P, D])
        A_sb = sb("A_sb", [P, NC, N])
        cst = sb("cst", [P, consts.shape[1]])
        ident = cst[:, 0:P]
        mean_m = cst[:, P:2 * P]
        row_col = cst[:, 2 * P:2 * P + 1]
        minus_half = cst[:, 2 * P + 1:2 * P + 2]
        eps_rms = cst[:, 2 * P + 2:2 * P + 3]
        lim0 = 2 * P + 3
        nlim = BLOCKS
        shift = sb("shift", [P, 1], U32)
        cw = sb("cw", [P, NC, TAPS])
        cb = sb("cb", [P, NC])
        dtb = sb("dtb", [P, NC])
        dpar = sb("dpar", [P, NC])
        lnw = sb("lnw", [P, 1])
        carry = sb("carry", [P, NC * N])
        halo = sb("halo", [P, NC, HALO])
        st6 = sb("st6", [P, KT, 6])
        mv = sb("mv", [P, KT, 2])
        rstd = sb("rstd", [P, KT])
        nmr = sb("nmr", [P, KT])

        ps = ctx.enter_context(nc.psum_tensor("ps", [P, 8, T], F32))
        acc = ps[:, 0:4, :]
        PB = [ps[:, 4, :], ps[:, 5, :]]
        Y = ps[:, 6, :]
        M = ps[:, 7, :]

        const_full = sem("const_full"); vec_full = sem("vec_full")
        zeroed = sem("zeroed")
        win_full = [sem("win_full0"), sem("win_full1")]; wout_full = sem("wout_full"); wsmall_full = sem("wsmall_full")
        words_full = sem("words_full"); dwords_full = sem("dwords_full")
        scale_full = sem("scale_full"); dscale_full = sem("dscale_full")
        scale_split = sem("scale_split"); dscale_split = sem("dscale_split")
        prep_mm = sem("prep_mm"); prep_hi = sem("prep_hi"); prep_w = sem("prep_w"); prep_lo = sem("prep_lo")
        small_t = sem("small_t"); small_copied = sem("small_copied")
        stored = [sem(f"stored{k}") for k in range(4)]
        a_full = [sem(f"a_full{k}") for k in range(NA)]
        b_full = [sem(f"b_full{k}") for k in range(NBR)]
        wx_done = sem("wx_done")
        p_full = sem("p_full"); p_read = [sem("p_read0"), sem("p_read1")]
        exp_done = sem("exp_done"); dbu_done = sem("dbu_done"); scan_done = sem("scan_done")
        p_done = sem("p_done"); pair_added = sem("pair_added"); nsum_done = sem("nsum_done")
        bb_full = [sem(f"bb_full{g}") for g in range(SPC)]
        cb_full = [sem(f"cb_full{g}") for g in range(SPC)]
        bc_stored = sem("bc_stored")
        sp_ready = sem("sp_ready"); delta_ready = sem("delta_ready"); du_ready = sem("du_ready")
        ud_ready = sem("ud_ready"); y_added = sem("y_added"); y_gated = sem("y_gated")
        yh_ready = sem("yh_ready"); yl_ready = sem("yl_ready"); wout_done = sem("wout_done")
        gate_ready = sem("gate_ready")
        h_ready = sem("h_ready"); hh_ready = sem("hh_ready"); hl_ready = sem("hl_ready")
        down_done = sem("down_done")
        ln_full = sem("ln_full"); ln_var = sem("ln_var"); ln_pow = sem("ln_pow")
        ln_stats = sem("ln_stats"); ln_norm = sem("ln_norm")
        xh_ready = sem("xh_ready"); xt_ready = sem("xt_ready")
        cv_ready = sem("cv_ready"); ue_ready = sem("ue_ready"); u_ready = sem("u_ready")
        sq_ready = sem("sq_ready"); xdn_ready = sem("xdn_ready")
        rows_full = sem("rows_full"); rows_added = sem("rows_added"); rows_left = sem("rows_left")
        vec_link = sem("vec_link"); act_link = sem("act_link")

        def step_no(i, s):
            return STEPS * i + (STEPS + s + 1)

        def chunk_no(i, c):
            return NC * i + (NC + c + 1)

        def added_no(i, s):
            return sum(PREADD) * i + sum(PREADD[k] if k >= 0 else 0 for k in range(s + 1)) if s >= 0 else (
                sum(PREADD) * i - sum(PREADD[k] for k in range(STEPS + s + 1, STEPS)))

        def limit(base, m):
            return cst[:, base:base + 1] if m is FIRST else cst[:, bass.ds(m + base, 1)]

        def wait(eng, semaphore, count):
            if not (isinstance(count, int) and count <= 0):
                eng.wait_ge(semaphore, count)

        def iteration(i, kind):
            back = kind in AHEAD
            return (0, -1) if i is None else (i, -back)

        def psum_at(i, shift, kind):
            pos = PSUM_ORDER.index(kind)
            bank, size = pos % 2, len(PSUM_ORDER)
            per = len(range(bank, size, 2))
            prologue = len([k for k in range(PSUM_PRE, size) if k % 2 == bank])
            return (bank, size * i + (size * shift + size - PSUM_PRE + pos + 1),
                    per * i + (per * shift + prologue + pos // 2 + 1))

        def psum_use(i, kind):
            return psum_at(*iteration(i, kind), kind)

        def psum_free(eng, i, kind):
            bank, _, nth = psum_use(i, kind)
            wait(eng, p_read[bank], nth - 1)

        def fill(ring, pre, slots, i, shift, kind):
            pos = ring.index(kind)
            per = len(ring) // slots
            prologue = len([k for k in range(pre, len(ring)) if k % slots == pos % slots])
            left_out = (len([k for k in range(pos % slots, pos, slots) if ring[k] in FOR_NEXT])
                        if isinstance(i, int) and i + shift == LAST else 0)
            return pos % slots, per * i + (per * shift + prologue + pos // slots + 1 - left_out)

        def unit_slot(eng, i, kind):
            if kind in RING_A:
                slot, times = fill(RING_A, A_PRE, NA, *iteration(i, kind), kind)
                eng.wait_ge(a_full[slot], 16 * times)
                return ring_a, slot
            slot, times = fill(RING_B, B_PRE, NBR, *iteration(i, kind), kind)
            eng.wait_ge(b_full[slot], 16 * times)
            return ring_b, slot

        WORDS = 2 * F * KT
        win_tiles = [ssm[:, 0:NC * HID].rearrange("p (r h) -> p r h", r=NC), u]
        words = bc_all[:, 0:WORDS].bitcast(U32).rearrange("p (k f) -> p k f", k=KT)
        wout_nat = bc_all[:, WORDS:WORDS + HID // P * D].rearrange("p (f d) -> p f d", f=HID // P)
        dword_tiles = [u, wout_nat[:, 0:HID // P, 0:HID]]
        dwords = [dword_tiles[j // NC][:, j % NC, :].bitcast(U32) for j in range(NF)]
        didx = u_raw[:].rearrange("p b t -> p (b t)")[0:G_D, 0:F]
        sc_raw = ssm[0:G_GU, 0:2 * F]
        z_int = ssm[0:G_GU, 2 * F:4 * F].bitcast(U32)
        qz_raw = ssm[0:G_GU, 4 * F:4 * F + F // 4].bitcast(U32)
        gidx = ffn_e[0:G_GU, :]
        dsc_raw = ffn_u[0:G_D, :]
        dz_int = ffn_g[0:G_D, :].bitcast(U32)
        dqz_raw = gate[0:G_D, NGATE - 1, 0:HID // 8].bitcast(U32)
        wx_nat = delta[0:XP, 0:2, :].rearrange("p a t -> p (a t)")
        wdt_nat = du[:, 0, 0:NC * R].rearrange("p (c r) -> p c r", c=NC)
        LOW = 32
        xT_flat = xT[:].rearrange("p a k t -> p (a k t)")
        ra_flat = ring_a[:].rearrange("p s a t -> p (s a t)")
        rb_flat = ring_b[:].rearrange("p s a t -> p (s a t)")
        sc_parts, z_rows, pick = xT_flat[:, 0:2 * F], rb_flat[:, 0:2 * F], h_hl[:, 0, :]
        dsc_parts, dz_rows, dpick = y_hl[:, 0, :], h_hl[:, 1, :], ra_flat[:, 0:F]
        stage = [t.rearrange("p (a t) -> p a t", a=2) for t in
                 (xT_flat[:, 3 * 2 * T:4 * 2 * T], ra_flat[:, 2 * 2 * T:3 * 2 * T],
                  ssm[:, (NDA + NHB - 1) * 2 * T:].bitcast(F32R),
                  delta[:, 2:4, :].bitcast(F32R).rearrange("p a t -> p (a t)"))]
        STAGES = len(stage)
        w_int, w_deq = [ud[:, 0, :], ud[:, 1, :]], [sp_l[:, 0, :], sp_l[:, 1, :]]
        ZEROED = 10
        lnx = [conv[:, 0, :], conv[:, 1, :], conv[:, 2, :], e_cg[:]]
        DEQ = 3 * NC

        def unit_view(tile, n):
            kind, k = KIND[n]
            if kind in ("g", "up") and width(k) < P:
                return tile.rearrange("p a (k f) -> p a k f", k=KT)[:, :, :, 0:width(k)]
            if kind == "down":
                return tile[0:width(k)]
            return tile

        def unit_dram(n):
            return unit_view(units[n].rearrange("p (a t) -> p a t", a=2), n)

        def unit_used(sp, i, shift, kind):
            if kind[0] == "down":
                wait(sp, down_done, NF * i + (NF * shift + kind[1] + 1))
            elif kind == ("wout", NC - 1):
                wait(sp, wout_done, chunk_no(i, NC * shift + NC - 1))
            elif kind[0] == "wout":
                wait(sp, wout_done, chunk_no(i, NC * shift + kind[1]))
            else:
                wait(sp, p_full, psum_at(i, shift, kind)[1])

        def load_down_words(sp):
            full = F // P
            for r in range(8):
                for tile, lo, hi in ((dword_tiles[0], 0, NC), (dword_tiles[1], NC, full)):
                    sp.dma_start(tile[r:P:8, 0:hi - lo, :].bitcast(U32),
                                 qw_d[P // 8 * lo:P // 8 * hi, :].rearrange("(j w) f -> w j f", w=P // 8)
                                 ).then_inc(dwords_full, 16)
                sp.dma_start(dwords[full][r:F - full * P:8, :], qw_d[P // 8 * full:, :]).then_inc(dwords_full, 16)

        def out_project(pe, into_acc, i, c):
            _, slot = unit_slot(pe, i, ("wout", c % NC))
            pe.wait_ge(yl_ready, chunk_no(i, c))
            into_acc(ring_a, slot, P, y_hl, wout_done, last_of_block=c == -1)

        block = ctx.enter_context(nc.Block())

        @block.sync
        def _(sp):
            def load_x(m, block_no):
                for t in range(KT):
                    sp.dma_start(lnx[t], x_tok[block_no, t]).then_inc(ln_full, 16)

            win_v = W_in.rearrange("(r p) h -> p r h", p=P)
            sp.dma_start(cst[:], consts).then_inc(const_full, 16)
            sp.dma_start(win_tiles[0], win_v[:, 0:NC, :]).then_inc(win_full[0], 16)
            sp.dma_start(u[:], win_v[:, NC:2 * NC, :]).then_inc(win_full[1], 16)
            sp.dma_start(wout_nat, W_out.rearrange("(f p) d -> p f d", p=P)).then_inc(wout_full, 16)
            load_x(FIRST, 0)
            for n in range(UNITS):
                if n == NC:
                    sp.wait_ge(prep_mm, NC)
                    sp.dma_start(sc_raw, sc_gu).then_inc(scale_full, 16)
                    sp.dma_start(qz_raw, qz_gu).then_inc(scale_full, 16)
                    for r in range(8):
                        sp.dma_start(words[r:P:8, :, :],
                                     qw_gu.rearrange("(k w) f -> w k f", k=KT)).then_inc(words_full, 16)
                if n == DEQ + 1:
                    sp.wait_ge(prep_mm, DEQ)
                    load_down_words(sp)
                sp.wait_ge(prep_lo, n + 1)
                sp.dma_start(unit_dram(n), unit_view(stage[n % STAGES].bitcast(F32), n)).then_inc(stored[n % STAGES], 16)
            for k in range(STAGES):
                sp.wait_ge(stored[k], 16 * len(range(k, UNITS, STAGES)))

            def load(i, shift, kind):
                ring, pre, slots, tile, full = ((RING_A, A_PRE, NA, ring_a, a_full) if kind in RING_A
                                                else (RING_B, B_PRE, NBR, ring_b, b_full))
                pos, n = ring.index(kind), UNIT[kind]
                before = pos - slots
                while isinstance(i, int) and i + shift == LAST and before >= 0 and ring[before] in FOR_NEXT:
                    before -= slots
                if shift and ring[before][0] == "wout" and before >= pre:
                    sp.wait_ge(full[pos % slots], 16 * fill(ring, pre, slots, 0, -1, ring[before])[1])
                elif not (shift and before < pre):
                    unit_used(sp, i, shift - (before < 0), ring[before])
                sp.dma_start(unit_view(tile[:, pos % slots].bitcast(F32), n), unit_dram(n)).then_inc(
                    full[pos % slots], 16)

            for kind in ALL_ITEMS[ALL_ITEMS.index(("u", 0)):]:
                if kind in UNIT:
                    load(0, -1, kind)
            for kind in RING_A[-NA:]:
                if kind[0] == "wout":
                    slot, times = fill(RING_A, A_PRE, NA, 0, -1, kind)
                    sp.wait_ge(a_full[slot], 16 * times)
            def iteration_loads(i, final=False):
                for s in ITERATION:
                    if s == ROWS_STEP:
                        if final:
                            sp.wait_ge(rows_left, 16 * KT * i + 16)
                        else:
                            sp.wait_ge(u_ready, NC * i + 2 * NC)
                        for t in range(KT):
                            sp.dma_start(lnx[t], x_tok[i, t]).then_inc(rows_full, 16)
                    if s == LOAD_X_STEP and not final:
                        sp.wait_ge(rows_left, 16 * KT * i + 16)
                        load_x(i + 1, i + 1)
                    for kind in items(s):
                        if kind in UNIT and not (final and kind in FOR_NEXT):
                            load(i, 0, kind)

            with sp.Fori(0, LAST) as i:
                iteration_loads(i)
            iteration_loads(LAST, True)

        @block.tensor
        def _(pe):
            def parts3(psum, stat, mov, start, stop):
                for k, (a, b) in enumerate(((0, 0), (0, 1), (1, 0))):
                    last = nc.tensor.matmul(psum, stat(a), mov(b), start=start and k == 0, stop=stop and k == 2,
                                            skip_group_check=True)
                return last

            pe.wait_ge(const_full, 16)
            pe.wait_ge(wsmall_full, 32)
            for c in range(NC):
                last = nc.tensor.transpose(ps[:, 4, c * XP:(c + 1) * XP], wx_nat[:, c * P:(c + 1) * P],
                                           ident[0:XP, 0:XP])
            for c in range(NC):
                last = nc.tensor.transpose(ps[0:R, 5 + c // 4, c % 4 * P:(c % 4 + 1) * P], wdt_nat[:, c, :], ident)
            last.then_inc(small_t, 1)
            for n in range(UNITS):
                kind, k = KIND[n]
                if n in (0, NC):
                    pe.wait_ge(win_full[n // NC], 16)
                if n == 2 * NC:
                    pe.wait_ge(wout_full, 16)
                if n == DEQ:
                    pe.wait_ge(scale_split, 1)
                    pe.wait_ge(small_copied, 1)
                if n == DEQ + 2 * NF:
                    pe.wait_ge(dscale_split, 1)
                if n >= 4:
                    if n - 4 < DEQ:
                        pe.wait_ge(prep_lo, n - 3)
                    else:
                        pe.wait_ge(prep_w, n - 3 - DEQ)
                w = width(k) if kind in ("g", "up", "down") else P
                for f in range(KT):
                    bank = ps[:, n % 4, f * P:(f + 1) * P]
                    if kind in ("u", "gate"):
                        last = nc.tensor.transpose(bank, win_tiles[n // NC][:, n % NC, f * P:(f + 1) * P], ident)
                    elif kind == "wout":
                        last = nc.tensor.transpose(bank, wout_nat[:, f, k * P:(k + 1) * P], ident)
                    elif kind in ("g", "up"):
                        col = (kind == "up") * F + k * P
                        rows = pick[:, f * P:(f + 1) * P]
                        nc.tensor.matmul(ps[:, n % 4, f * P:f * P + w], rows, sc_parts[:, col:col + w],
                                         start=True, stop=True)
                        last = nc.tensor.matmul(ps[:, 4 + n % 4, f * P:f * P + w], rows, z_rows[:, col:col + w],
                                                start=True, stop=True)
                if kind == "down":
                    rows = dpick[:, k * P:k * P + w]
                    nc.tensor.matmul(ps[0:w, n % 4, :], rows, dsc_parts, start=True, stop=True)
                    last = nc.tensor.matmul(ps[0:w, 4 + n % 4, :], rows, dz_rows, start=True, stop=True)
                last.then_inc(prep_mm, 1)
            pe.wait_ge(prep_lo, UNITS)
            pe.sem_inc(nsum_done, STEPS)
            pe.sem_inc(wout_done, NC)

            def project(i, kind, bank, w):
                ring, slot = unit_slot(pe, i, kind)
                psum_free(pe, i, kind)
                for f in range(KT):
                    last = parts3(PB[bank][0:w, :], lambda a: ring[:, slot, a, f * P:f * P + w],
                                  lambda b: xT[:, b, f, :], f == 0, f == KT - 1)
                last.then_inc(p_full, 1)

            def into_acc(ring, slot, rows, hl, done, first=False, last_of_block=False):
                for t in range(KT):
                    last = parts3(acc[:, t, :], lambda a: hl[0:rows, a, t * P:(t + 1) * P],
                                  lambda b: ring[0:rows, slot, b, :], first, last_of_block)
                last.then_inc(done, 1)

            def transposes(i, t):
                kind = ("xt", t)
                bank, _, _ = psum_use(i, kind)
                psum_free(pe, i, kind)
                for f in range(KT):
                    last = nc.tensor.transpose(PB[bank][:, f * P:(f + 1) * P], lnx[t][:, f * P:(f + 1) * P], ident)
                last.then_inc(p_full, 1)

            def x_project(m, c):
                if c == 0:
                    wait(pe, xdn_ready, m)
                pe.wait_ge(u_ready, NC * m + (c + 1))
                last = nc.tensor.matmul(M[0:XP, :], WxT[:, c, :], u[:, c, :], start=(c == 0), stop=(c == NC - 1),
                                        skip_group_check=True)
                if c == NC - 1:
                    last.then_inc(wx_done, 1)

            def mean_squares(i, m):
                bank, _, _ = psum_use(i, ("ms", 0))
                psum_free(pe, i, ("ms", 0))
                pe.wait_ge(sq_ready, m + 1)
                nc.tensor.matmul(PB[bank], mean_m[0:XP, :], sp_l[0:XP, 0, :], start=True, stop=True,
                                 skip_group_check=True).then_inc(p_full, 1)

            def delta_rows(i, c, m):
                bank, _, _ = psum_use(i, ("dtz", c))
                psum_free(pe, i, ("dtz", c))
                if m is not None:
                    pe.wait_ge(xdn_ready, m + 1)
                nc.tensor.matmul(PB[bank], WdtT[:, c * P:(c + 1) * P], xdn[:], start=True, stop=True,
                                 skip_group_check=True).then_inc(p_full, 1)

            def state_sum(i, s):
                c, g = divmod(s, SPC)
                if PREADD[s]:
                    pe.wait_ge(pair_added, added_no(i, s))
                else:
                    pe.wait_ge(p_done, step_no(i, s))
                if g == 0:
                    pe.wait_ge(y_added, chunk_no(i, c - 1))
                pairs = 1 if PREADD[s] else PAIR
                for k in range(pairs):
                    last = nc.tensor.matmul(Y, ident, dA[:, DA_SLOT[s], k, :], start=(g == 0 and k == 0),
                                            stop=(g == SPC - 1 and k == pairs - 1), skip_group_check=True)
                last.then_inc(nsum_done, 1)

            def mlp(i, s):
                for kind in block_items(s):
                    bank, _, _ = psum_use(i, kind)
                    project(i, kind, bank, width(kind[1]) if kind[0] in ("g", "up") else P)

            def front(i, m, s):
                for t in at(XT_STEP, s):
                    if t == 0:
                        pe.wait_ge(ln_norm, m + 1)
                    transposes(i, t)
                for c in at(U_STEP, s):
                    if c == 0:
                        pe.wait_ge(xt_ready, KT * m + KT)
                    bank, _, _ = psum_use(i, ("u", c))
                    project(i, ("u", c), bank, P)
                for c in at(WX_STEP, s):
                    x_project(m, c)
                if s == MS_STEP:
                    mean_squares(i, m)
                if s == DTZ0_STEP:
                    delta_rows(i, 0, m)
                    delta_rows(i, 1, m)

            def step(i, s, first=False, final=False):
                if not first or s >= SUM_LAG:
                    state_sum(i, s - SUM_LAG)
                mlp(i, s)
                for k in (0, 1):
                    for q in at(DTZ_STEP, s - k):
                        delta_rows(i, 2 * q + 2 + k, None)
                for j in at(DOWN_STEP, s):
                    _, slot = unit_slot(pe, i, ("down", j))
                    pe.wait_ge(hl_ready, NF * i + (j + 1))
                    if j == 0:
                        pe.wait_ge(rows_added, KT * i + KT)
                    into_acc(ring_b, slot, width(j), h_hl, down_done, first=j == 0)
                if s >= HEAD and not final:
                    front(i, i + 1, s)
                for c in at(WOUT_STEP, s):
                    if c < NC - 1:
                        out_project(pe, into_acc, i, c)
                    elif not first:
                        out_project(pe, into_acc, i, -1)
                if s - STEPS >= EARLY and not final:
                    mlp(i + 1, s - STEPS)

            for s in range(XT_STEP[0], STEPS):
                front(None, FIRST, s)
                if s - STEPS >= EARLY:
                    mlp(0, s - STEPS)
            for s in range(HEAD):
                step(0, s, True)
            with pe.Fori(0, LAST) as i:
                for s in range(HEAD, STEPS):
                    step(i, s)
                for s in range(HEAD):
                    step(i + 1, s)
            for s in range(HEAD, STEPS):
                step(LAST, s, final=True)
            for s in range(STEPS - SUM_LAG, STEPS):
                state_sum(LAST, s)
            out_project(pe, into_acc, BLOCKS, -1)

        @block.scalar
        def _(act):
            links = [0, 0]

            def link(ins, i):
                links[i is not None] += 1
                ins.then_inc(act_link, 1)
                n = links[i is not None]
                act.wait_ge(act_link, n if i is None else ACT_LINKS * i + (links[0] + n))

            act.dma_start(wx_nat, Wx).then_inc(wsmall_full, 16)
            act.dma_start(wdt_nat, Wdt.rearrange("(c p) r -> p c r", p=P)).then_inc(wsmall_full, 16)
            act.dma_start(gidx.bitcast(I32), idx_gu.unsqueeze(0).broadcast_to([G_GU, HID])).then_inc(scale_full, 16)
            act.dma_start(didx.bitcast(I32), idx_d.unsqueeze(0).broadcast_to([G_D, F])).then_inc(dscale_full, 16)
            act.dma_start(dsc_raw, sc_d).then_inc(dscale_full, 16)
            act.dma_start(dqz_raw, qz_d).then_inc(dscale_full, 16)
            act.dma_start(cw[:], conv_w.rearrange("(c p) k -> p c k", p=P)).then_inc(vec_full, 16)
            for tile, vec in ((cb, conv_b), (dtb, dt_bias), (dpar, D_param)):
                act.dma_start(tile[:], vec.rearrange("(c p) -> p c", p=P),
                              allow_slow_non_contiguous=True).then_inc(vec_full, 16)
            act.dma_start(A_sb[:], A.rearrange("(c p) n -> p c n", p=P)).then_inc(vec_full, 16)
            for lo, hi, vec in ((0, R, dt_ln_w), (R, R + N, b_ln_w), (R + N, XP, c_ln_w)):
                act.dma_start(lnw[lo:hi, :], vec.unsqueeze(1)).then_inc(vec_full, 16)
            act.wait_ge(small_t, 1)
            act.wait_ge(zeroed, ZEROED)
            nc.scalar.copy(WxT[:].rearrange("p c m -> p (c m)"), ps[:, 4, :])
            nc.scalar.copy(WdtT[0:R, :].rearrange("p (h d) -> p h d", h=2), ps[0:R, 5:7, :]).then_inc(small_copied, 1)

            def layer_norm(m):
                act.wait_ge(ln_stats, m + 1)
                for t in range(KT):
                    last = nc.scalar.activation(lnx[t], lnx[t], ACT.Identity, bias=nmr[:, t:t + 1],
                                                scale=rstd[:, t:t + 1])
                last.then_inc(ln_norm, 1)

            for n in range(UNITS):
                if n == NC:
                    layer_norm(FIRST)
                if n < DEQ:
                    act.wait_ge(prep_mm, n + 1)
                    src = ps[:, n % 4, :].rearrange("p (a t) -> p a t", a=1)
                else:
                    act.wait_ge(prep_w, n - DEQ + 1)
                    src = w_deq[n % 2].rearrange("p (a t) -> p a t", a=1)
                if n >= STAGES:
                    act.wait_ge(stored[n % STAGES], 16 * (n // STAGES))
                nc.scalar.copy(unit_view(stage[n % STAGES][:, 0:1, :], n), unit_view(src, n)).then_inc(prep_hi, 1)
            act.sem_inc(exp_done, STEPS)
            act.sem_inc(ud_ready, NC)
            act.sem_inc(yh_ready, NC)
            act.sem_inc(rows_left, 16)

            def x_high(i, t):
                bank, full, _ = psum_use(i, ("xt", t))
                act.wait_ge(p_full, full)
                nc.scalar.copy(xT[:, 0, :, t * P:(t + 1) * P],
                               PB[bank].rearrange("p (k t) -> p k t", k=KT)).then_inc(xh_ready, 1)

            def u_evacuate(i, m, c):
                bank, full, _ = psum_use(i, ("u", c))
                act.wait_ge(p_full, full)
                if m is not FIRST or c >= NCV:
                    act.wait_ge(u_ready, NC * m + (c - NCV + 1))
                nc.scalar.copy(u_raw[:, c % NCV, HALO:], PB[bank])
                nc.scalar.activation(conv[:, c % NCV, :], PB[bank], ACT.Identity, bias=cb[:, c:c + 1],
                                     scale=cw[:, c, TAPS - 1:TAPS]).then_inc(p_read[bank], 1)

            def u_tanh(i, m, c):
                act.wait_ge(cv_ready, NC * m + (c + 1))
                if m is not FIRST or c >= 1:
                    act.wait_ge(u_ready, NC * m + c)
                link(nc.scalar.activation(e_cg[:], conv[:, c % NCV, :], ACT.Tanh), i)
                nc.scalar.activation(e_cg[:], e_cg[:], ACT.Copy, bias=1.0).then_inc(ue_ready, 1)

            def squares(m):
                act.wait_ge(wx_done, m + 1)
                if m is not FIRST:
                    act.wait_ge(delta_ready, NC // 2 * m)
                nc.scalar.activation(sp_l[0:XP, 0, :], M[0:XP, :], ACT.Square).then_inc(sq_ready, 1)

            def root_mean(i, m):
                bank, full, _ = psum_use(i, ("ms", 0))
                act.wait_ge(p_full, full)
                nc.scalar.activation(sp_l[0:XP, 0, :], PB[bank][0:XP, :], ACT.Sqrt,
                                     bias=eps_rms[0:XP, :]).then_inc(p_read[bank], 1)

            def store_bc(m):
                act.wait_ge(xdn_ready, m + 1)
                act.dma_start(bc_dram, xdn[R:XP, :]).then_inc(bc_stored, 16)

            def softplus_in(i, c, pairs, chunks):
                if i is not None:
                    act.wait_ge(delta_ready, pairs)
                    act.wait_ge(du_ready, chunks)
                bank, full, _ = psum_use(i, ("dtz", c))
                act.wait_ge(p_full, full)
                nc.scalar.activation(delta[:, c % 4, :], PB[bank], ACT.Identity, bias=dtb[:, c:c + 1])
                nc.scalar.activation(sp_l[:, c % 2, :], PB[bank], ACT.Abs,
                                     bias=dtb[:, c:c + 1]).then_inc(p_read[bank], 1)

            def softplus(i, q):
                for c in (2 * q, 2 * q + 1):
                    bank, _, read = psum_use(i, ("dtz", c))
                    act.wait_ge(p_read[bank], read)
                link(nc.scalar.activation(sp_l[:], sp_l[:], ACT.Exp, scale=-1.0), i)
                nc.scalar.activation(sp_l[:], sp_l[:], ACT.Ln, bias=1.0).then_inc(sp_ready, 1)

            def skip(i, c):
                act.wait_ge(yl_ready, chunk_no(i, c - 2))
                act.wait_ge(u_ready, NC * i + (c + 1))
                nc.scalar.activation(ud[:, c % 2, :], u[:, c % NC, :], ACT.Copy,
                                     scale=dpar[:, c % NC:c % NC + 1]).then_inc(ud_ready, 1)

            def y_high(i, c):
                act.wait_ge(y_gated, chunk_no(i, c))
                act.wait_ge(wout_done, chunk_no(i, c - 1))
                nc.scalar.copy(y_hl[:, 0, :], ud[:, c % 2, :]).then_inc(yh_ready, 1)

            def broadcast(i, rows, tile, g, full):
                act.dma_start(tile[:, g * PAIR:(g + 1) * PAIR, :],
                              bc_dram[rows + g * PAIR:rows + (g + 1) * PAIR, :].partition_broadcast(P)
                              ).then_inc(full[g], 16)

            def rows(i, g):
                act.wait_ge(dbu_done, step_no(i, g - SPC))
                broadcast(i, 0, B_bc, g, bb_full)
                act.wait_ge(p_done, step_no(i, g - SPC))
                broadcast(i, N, C_bc, g, cb_full)

            def rows_leave(i):
                for t in range(KT):
                    act.wait_ge(rows_added, KT * i + (t + 1))
                    act.dma_start(out_tok[loop_block[0], t], lnx[t]).then_inc(rows_left, 16)

            def decay(i, s):
                c, g = divmod(s, SPC)
                if g == 0:
                    act.wait_ge(delta_ready, NC // 2 * i + (c // 2 + 1))
                act.wait_ge(nsum_done, step_no(i, s - since(DA_SLOT, s)))
                for k in range(PAIR):
                    last = nc.scalar.activation(dA[:, DA_SLOT[s], k, :], delta[:, c % 4, :], ACT.Exp,
                                                scale=A_sb[:, c, g * PAIR + k:g * PAIR + k + 1])
                last.then_inc(exp_done, 1)

            def tanh_buffer_free(i, kind):
                pos = E_ORDER.index(kind)
                before, n = E_ORDER[pos - 1]
                if before == "g":
                    wait(act, h_ready, NF * i + (n + 1 - NF * (pos == 0)))
                else:
                    act.wait_ge(gate_ready, chunk_no(i, n - NC * (pos == 0)))

            def mlp(i, s):
                for j in at(G_STEP, s - 1):
                    w = width(j)
                    bank, full, _ = psum_use(i, ("g", j))
                    act.wait_ge(p_full, full)
                    wait(act, h_ready, NF * i + j)
                    tanh_buffer_free(i, ("g", j))
                    nc.scalar.activation(ffn_e[0:w, :], PB[bank][0:w, :], ACT.Tanh, scale=0.5)
                    nc.scalar.mul(ffn_g[0:w, :], PB[bank][0:w, :], 0.5).then_inc(p_read[bank], 1)
                for j in at(UP_STEP, s - 1):
                    w = width(j)
                    bank, full, _ = psum_use(i, ("up", j))
                    act.wait_ge(p_full, full)
                    wait(act, hl_ready, NF * i + j)
                    nc.scalar.copy(ffn_u[0:w, :], PB[bank][0:w, :]).then_inc(p_read[bank], 1)
                for j in at(HIGH_STEP, s):
                    w = width(j)
                    act.wait_ge(h_ready, NF * i + (j + 1))
                    wait(act, down_done, NF * i + j)
                    nc.scalar.copy(h_hl[0:w, 0, :], ffn_u[0:w, :]).then_inc(hh_ready, 1)
                for c in at(GATE_STEP, s - 1):
                    bank, full, _ = psum_use(i, ("gate", c))
                    act.wait_ge(p_full, full)
                    tanh_buffer_free(i, ("gate", c))
                    act.wait_ge(y_gated, chunk_no(i, c - NGATE))
                    nc.scalar.activation(ffn_e[:], PB[bank], ACT.Tanh, scale=0.5)
                    nc.scalar.mul(gate[:, c % NGATE, :], PB[bank], 0.5).then_inc(p_read[bank], 1)

            def front(i, m, s):
                for t in at(XT_STEP, s - 1):
                    x_high(i, t)
                for c in at(U_STEP, s - 1):
                    u_evacuate(i, m, c)
                for c in at(U_STEP, s - 3):
                    u_tanh(i, m, c)
                if s == MS_STEP:
                    squares(m)
                    root_mean(i, m)
                if s == DTZ0_STEP:
                    store_bc(m)
                if s == DTZ0_STEP + 1:
                    softplus_in(i, 0, NC // 2 * m, NC * m - 2)
                    softplus_in(i, 1, NC // 2 * m, NC * m - 2)
                    softplus(i, 0)
                if s == DTZ0_STEP + 2:
                    act.wait_ge(bc_stored, 16 * (m + 1))
                    rows(m, 0)
                    rows(m, 1)

            def step(i, s, first=False, final=False):
                c, g = divmod(s, SPC)
                if s + 2 < SPC:
                    rows(i, s + 2)
                if s + EXP_LEAD < STEPS:
                    decay(i, s + EXP_LEAD)
                elif not final:
                    decay(i + 1, s + EXP_LEAD - STEPS)
                if g == 4 and not (first and c == 0):
                    y_high(i, c - 1)
                if g == 6 and not (final and c == NC - 1):
                    skip(i, c + 1)
                mlp(i, s)
                for k in (0, 1):
                    for q in at(DTZ_STEP, s - 1 - k):
                        softplus_in(i, 2 * q + 2 + k, NC // 2 * i + (q + 1), NC * i + max(2 * q, 1))
                for q in at(DTZ_STEP, s - 3):
                    softplus(i, q + 1)
                if s == LN_STEP + 2 and not final:
                    layer_norm(i + 1)
                if s >= HEAD and not final:
                    front(i, i + 1, s)
                if s - STEPS >= EARLY and not final:
                    mlp(i + 1, s - STEPS)
                if s == HEAD - 1 and not first:
                    rows_leave(i)

            for k in range(STAGES):
                act.wait_ge(stored[k], 16 * len(range(k, UNITS, STAGES)))
            for s in range(XT_STEP[0], STEPS):
                front(None, FIRST, s)
                if s - STEPS >= EARLY:
                    mlp(0, s - STEPS)
            skip(0, 0)
            for s in range(EXP_LEAD):
                decay(0, s)
            loop_block = [None]
            for s in range(HEAD):
                step(0, s, True)
            with act.Fori(0, LAST) as i:
                links[1] = 0
                loop_block[0] = i
                for s in range(HEAD, STEPS):
                    step(i, s)
                for s in range(HEAD):
                    step(i + 1, s)
            assert links[1] == ACT_LINKS, links
            links[1], loop_block[0] = 0, LAST
            for s in range(HEAD, STEPS):
                step(LAST, s, final=True)
            y_high(BLOCKS, -1)
            rows_leave(BLOCKS)
            act.wait_ge(rows_left, 16 * KT * BLOCKS + 16)
            act.wait_ge(bc_stored, 16 * BLOCKS)

        @block.gpsimd
        def _(pool):
            for tile in (sc_parts, z_rows, pick, dsc_parts, dz_rows, dpick, WdtT[:], xdn[:], carry[:], halo[:]):
                nc.gpsimd.memset(tile.bitcast(F32), 0.0).then_inc(zeroed, 1)

            def rsqrt_var(m):
                pool.wait_ge(ln_var, m + 1)
                nc.gpsimd.tensor_tensor(rstd[:], rstd[:], minus_half.broadcast_to([P, KT]),
                                        ALU.pow).then_inc(ln_pow, 1)

            rsqrt_var(FIRST)
            for n in range(DEQ, UNITS):
                pool.wait_ge(prep_hi, n + 1)
                nc.gpsimd.tensor_tensor(unit_view(stage[n % STAGES][:, 1:2, :], n),
                                        unit_view(w_deq[n % 2].rearrange("p (a t) -> p a t", a=1), n),
                                        unit_view(stage[n % STAGES][:, 0:1, :], n).bitcast(F32),
                                        ALU.subtract).then_inc(prep_lo, 1)
            pool.sem_inc(dbu_done, STEPS)
            pool.sem_inc(yl_ready, NC)

            def y_low(i, c):
                pool.wait_ge(yh_ready, chunk_no(i, c))
                nc.gpsimd.tensor_tensor(y_hl[:, 1, :], ud[:, c % 2, :], y_hl[:, 0, :].bitcast(F32),
                                        ALU.subtract).then_inc(yl_ready, 1)

            def mlp(i, s):
                for j in at(HIGH_STEP, s - 1):
                    w = width(j)
                    pool.wait_ge(hh_ready, NF * i + (j + 1))
                    nc.gpsimd.tensor_tensor(h_hl[0:w, 1, :], ffn_u[0:w, :], h_hl[0:w, 0, :].bitcast(F32),
                                            ALU.subtract).then_inc(hl_ready, 1)

            def u_silu(m, c):
                pool.wait_ge(ue_ready, NC * m + (c + 1))
                if m is not FIRST:
                    pool.wait_ge(ud_ready, NC * m + (c + 1))
                    pool.wait_ge(du_ready, NC * m + (c + 1 - NC))
                nc.gpsimd.tensor_tensor(u[:, c, :], e_cg[:], conv[:, c % NCV, :], ALU.mult).then_inc(u_ready, 1)

            def front(m, s):
                for c in at(U_STEP, s - 4):
                    u_silu(m, c)

            def pair_sum(i, s):
                if PREADD[s]:
                    pool.wait_ge(p_done, step_no(i, s))
                    nc.gpsimd.tensor_tensor(dA[:, DA_SLOT[s], 0, :], dA[:, DA_SLOT[s], 0, :], dA[:, DA_SLOT[s], 1, :],
                                            ALU.add).then_inc(pair_added, 1)

            def step(i, s, first=False, final=False):
                c, g = divmod(s, SPC)
                if g == 0:
                    pool.wait_ge(du_ready, NC * i + (c + 1))
                if c == 0:
                    pool.wait_ge(bb_full[g], 16 * (i + 1))
                pool.wait_ge(p_done, step_no(i, s - since(HB_SLOT, s)))
                nc.gpsimd.tensor_tensor(hb[:, HB_SLOT[s], :, :], B_bc[:, g * PAIR:(g + 1) * PAIR, :],
                                        du[:, c % 2, :].unsqueeze(1).broadcast_to([P, PAIR, T]),
                                        ALU.mult).then_inc(dbu_done, 1)
                if not first or s >= POOL_LAG:
                    pair_sum(i, s - POOL_LAG)
                if g == 5 and not (first and c == 0):
                    y_low(i, c - 1)
                mlp(i, s)
                if s == LN_STEP + 1 and not final:
                    rsqrt_var(i + 1)
                if s >= HEAD and not final:
                    front(i + 1, s)
                if s - STEPS >= EARLY and not final:
                    mlp(i + 1, s - STEPS)

            for s in range(XT_STEP[0], STEPS):
                front(FIRST, s)
                if s - STEPS >= EARLY:
                    mlp(0, s - STEPS)
            for s in range(HEAD):
                step(0, s, True)
            with pool.Fori(0, LAST) as i:
                for s in range(HEAD, STEPS):
                    step(i, s)
                for s in range(HEAD):
                    step(i + 1, s)
            for s in range(HEAD, STEPS):
                step(LAST, s, final=True)
            for s in range(STEPS - POOL_LAG, STEPS):
                pair_sum(LAST, s)
            y_low(BLOCKS, -1)

        @block.vector
        def _(dve):
            links = [0, 0]

            def link(ins, i=None):
                links[i is not None] += 1
                ins.then_inc(vec_link, 1)
                n = links[i is not None]
                dve.wait_ge(vec_link, n if i is None else VEC_LINKS * i + (links[0] + n))

            def group_rows(idx, groups, tmp, pick_rows, n, parts):
                link(nc.vector.tensor_scalar(tmp, idx.bitcast(I32), 0.0, float(groups), ALU.is_lt, ALU.mult))
                link(nc.vector.tensor_tensor(tmp, tmp, idx.bitcast(I32), ALU.add))
                link(nc.vector.tensor_scalar(tmp, tmp, 0.0, float(groups - 1), ALU.max, ALU.min))
                for lo in range(parts):
                    link(nc.vector.tensor_scalar(pick_rows[LOW * lo:LOW * lo + groups, :], tmp,
                                                 row_col[0:groups, :], None, ALU.is_equal))

            def scale_rows(raw, zero_words, zeros, groups, parts, rows):
                zv = zeros.rearrange("g (w k) -> g w k", k=8)
                for k in range(8):
                    last = nc.vector.tensor_scalar(zv[:, :, k], zero_words, 4 * k, 15, ALU.logical_shift_right,
                                                   ALU.bitwise_and)
                link(last)
                nc.vector.tensor_scalar(rows[0:groups, :], zeros, 1.0, None, ALU.add)
                link(nc.vector.tensor_copy(parts[0:groups, :], raw))
                nc.vector.tensor_tensor(parts[LOW:LOW + groups, :], raw, parts[0:groups, :].bitcast(F32),
                                        ALU.subtract)

            dve.wait_ge(const_full, 16)
            link(nc.vector.tensor_copy(shift[:], row_col))
            link(nc.vector.tensor_scalar(shift[:], shift[:], 7, 2, ALU.bitwise_and, ALU.logical_shift_left))
            dve.wait_ge(zeroed, ZEROED)

            def low_part(n):
                dve.wait_ge(prep_hi, n + 1)
                nc.vector.tensor_tensor(stage[n % STAGES][:, 1, :], ps[:, n % 4, :],
                                        stage[n % STAGES][:, 0, :].bitcast(F32), ALU.subtract).then_inc(prep_lo, 1)

            def ln_statistics(i, m):
                dve.wait_ge(ln_full, 16 * KT * (m + 1))
                for t in range(KT):
                    last = nc.vector.bn_stats(st6[:, t, :], lnx[t])
                link(last, i)
                nc.vector.memset(rstd[:], 0.0)
                for t in range(KT):
                    last = nc.vector.bn_aggr(mv[:, t, :], st6[:, t, :])
                link(last, i)
                nc.vector.tensor_scalar(rstd[:], mv[:, :, 1], EPS_LN, None, ALU.add).then_inc(ln_var, 1)

            def ln_bias(m):
                dve.wait_ge(ln_pow, m + 1)
                nc.vector.scalar_tensor_tensor(nmr[:], mv[:, :, 0], -1.0, rstd[:], ALU.mult,
                                               ALU.mult).then_inc(ln_stats, 1)

            for n in range(NC):
                low_part(n)
            ln_statistics(None, FIRST)
            ln_bias(FIRST)
            dve.wait_ge(vec_full, 16 * 8)
            nc.vector.tensor_scalar(cw[:], cw[:], 0.5, None, ALU.mult)
            link(nc.vector.tensor_scalar(cb[:], cb[:], 0.5, None, ALU.mult))
            dve.wait_ge(scale_full, 48)
            group_rows(gidx, G_GU, ffn_g[0:G_GU, :], pick, HID, 2)
            scale_rows(sc_raw, qz_raw, z_int, G_GU, sc_parts, z_rows)
            nc.vector.memset(st6[:], 0.0).then_inc(scale_split, 1)
            for n in range(NC, DEQ):
                low_part(n)
            for n in range(DEQ, UNITS):
                kind, k = KIND[n]
                w = width(k)
                d = n - DEQ
                if kind == "down" and k == 0:
                    dve.wait_ge(prep_lo, n)
                if kind == "down":
                    if k == 0:
                        dve.wait_ge(dwords_full, 16 * 8 * 3)
                    src = dwords[k][0:w, :]
                    wi = w_int[n % 2][0:w, :].bitcast(U32)
                    Z, S, W = ps[0:w, 4 + n % 4, :], ps[0:w, n % 4, :], w_deq[n % 2][0:w, :]
                else:
                    if d == 0:
                        dve.wait_ge(words_full, 128)
                    col = (kind == "up") * F + k * P
                    src = words[:, :, col:col + w]
                    wi, Z, S, W = (t.rearrange("p (k f) -> p k f", k=KT)[:, :, 0:w] for t in
                                   (w_int[n % 2].bitcast(U32), ps[:, 4 + n % 4, :], ps[:, n % 4, :],
                                    w_deq[n % 2]))
                rows = w if kind == "down" else P
                link(nc.vector.tensor_scalar(wi, src, shift[0:rows, :], 15, ALU.logical_shift_right,
                                             ALU.bitwise_and))
                dve.wait_ge(prep_mm, n + 1)
                link(nc.vector.tensor_tensor(wi.bitcast(F32), wi, Z, ALU.subtract))
                if d >= 2:
                    dve.wait_ge(prep_lo, n - 1)
                nc.vector.tensor_tensor(W, wi.bitcast(F32), S, ALU.mult).then_inc(prep_w, 1)
                if n == DEQ + 4:
                    dve.wait_ge(dscale_full, 48)
                    group_rows(didx, G_D, gate[0:G_D, 0:3, :].rearrange("p a t -> p (a t)")[:, 0:F], dpick, F, 2)
                    scale_rows(dsc_raw, dqz_raw, dz_int, G_D, dsc_parts, dz_rows)
                    nc.vector.memset(st6[:], 0.0).then_inc(dscale_split, 1)
            dve.sem_inc(scan_done, STEPS)
            dve.sem_inc(p_done, STEPS)
            dve.sem_inc(y_added, NC)
            dve.sem_inc(y_gated, NC)
            dve.sem_inc(gate_ready, NC)
            dve.sem_inc(rows_added, KT)

            def x_low(i, t):
                bank, _, _ = psum_use(i, ("xt", t))
                m_count = (t + 1) if i is None else KT * i + (KT + t + 1)
                dve.wait_ge(xh_ready, m_count)
                nc.vector.tensor_tensor(xT[:, 1, :, t * P:(t + 1) * P],
                                        PB[bank].rearrange("p (k t) -> p k t", k=KT),
                                        xT[:, 0, :, t * P:(t + 1) * P].bitcast(F32), ALU.subtract
                                        ).then_inc(p_read[bank], 1)
                if t == KT - 1:
                    for b in range(2):
                        bank, _, read = psum_use(i, ("xt", KT - 2 + b))
                        dve.wait_ge(p_read[bank], read)
                    dve.sem_inc(xt_ready, KT)

            def taps(i, m, c):
                bank, _, read = psum_use(i, ("u", c))
                dve.wait_ge(p_read[bank], read)
                link(nc.vector.tensor_scalar(u_raw[:, c % NCV, 0:HALO], halo[:, c, :],
                                             limit(lim0, m), limit(lim0 + nlim, m),
                                             ALU.min, ALU.max), i)
                nc.vector.tensor_copy(halo[:, c, :], u_raw[:, c % NCV, T:T + HALO])
                for k in range(TAPS - 1):
                    ins = nc.vector.scalar_tensor_tensor(conv[:, c % NCV, :], u_raw[:, c % NCV, k:k + T],
                                                         cw[:, c, k:k + 1], conv[:, c % NCV, :], ALU.mult, ALU.add)
                    if k < TAPS - 2:
                        link(ins, i)
                ins.then_inc(cv_ready, 1)

            def norm_rows(i, m):
                bank, _, read = psum_use(i, ("ms", 0))
                dve.wait_ge(p_read[bank], read)
                if m is not FIRST:
                    dve.wait_ge(bc_stored, 16 * m)
                link(nc.vector.reciprocal(sp_l[0:XP, 0, :], sp_l[0:XP, 0, :]), i)
                nc.vector.scalar_tensor_tensor(xdn[0:XP, :], M[0:XP, :], lnw[0:XP, 0:1], sp_l[0:XP, 0, :],
                                               ALU.mult, ALU.mult).then_inc(xdn_ready, 1)

            def delta_pair(pairs, q=0):
                dve.wait_ge(sp_ready, pairs + 1)
                z = delta[:, q % 2 * 2:q % 2 * 2 + 2, :]
                nc.vector.scalar_tensor_tensor(z, z, 0.0, sp_l[:], ALU.max, ALU.add).then_inc(delta_ready, 1)

            def du_rows(c, chunks, pairs):
                if chunks is not FIRST:
                    dve.wait_ge(dbu_done, SPC * chunks + (STEPS - SPC))
                dve.wait_ge(delta_ready, pairs + 1)
                dve.wait_ge(u_ready, chunks + 1)
                nc.vector.tensor_tensor(du[:, c % 2, :], delta[:, c % 4, :], u[:, c, :],
                                        ALU.mult).then_inc(du_ready, 1)

            def keep_state(i, s):
                c, g = divmod(s % STEPS, SPC)
                dve.wait_ge(scan_done, step_no(i, s))
                n = c * N + g * PAIR
                return nc.vector.tensor_copy(carry[:, n:n + PAIR], hb[:, HB_SLOT[s], :, T - 1])

            def times_c(i, s):
                c, g = divmod(s, SPC)
                if c == 0:
                    dve.wait_ge(cb_full[g], 16 * (i + 1))
                nc.vector.tensor_tensor(dA[:, DA_SLOT[s], :, :], hb[:, HB_SLOT[s], :, :],
                                        C_bc[:, g * PAIR:(g + 1) * PAIR, :], ALU.mult).then_inc(p_done, 1)

            loop_block = [None]

            def mlp(i, s):
                for j in at(UP_STEP, s - 1):
                    w = width(j)
                    for kind in (("g", j), ("up", j)):
                        bank, _, read = psum_use(i, kind)
                        dve.wait_ge(p_read[bank], read)
                    link(nc.vector.scalar_tensor_tensor(ffn_g[0:w, :], ffn_e[0:w, :], 1.0, ffn_g[0:w, :],
                                                        ALU.add, ALU.mult), loop_block[0])
                    nc.vector.tensor_tensor(ffn_u[0:w, :], ffn_g[0:w, :], ffn_u[0:w, :],
                                            ALU.mult).then_inc(h_ready, 1)
                for c in at(GATE_STEP, s - 1):
                    bank, _, read = psum_use(i, ("gate", c))
                    dve.wait_ge(p_read[bank], read)
                    nc.vector.scalar_tensor_tensor(gate[:, c % NGATE, :], ffn_e[:], 1.0, gate[:, c % NGATE, :],
                                                   ALU.add, ALU.mult).then_inc(gate_ready, 1)

            def front(i, m, s):
                for t in at(XT_STEP, s - 1):
                    x_low(i, t)
                for c in at(U_STEP, s - 2):
                    taps(i, m, c)
                if s == MS_STEP + 1:
                    norm_rows(i, m)
                if s == DTZ0_STEP + 2:
                    delta_pair(NC // 2 * m)
                if s == STEPS - 1:
                    du_rows(0, NC * m, NC // 2 * m)

            def add_rows(i):
                dve.wait_ge(rows_full, 16 * KT * i)
                dve.wait_ge(wout_done, chunk_no(i, -1))
                for t in range(KT):
                    nc.vector.tensor_tensor(lnx[t], acc[:, t, :], lnx[t], ALU.add).then_inc(rows_added, 1)

            def gated_y(i, c):
                dve.wait_ge(nsum_done, step_no(i, SPC * (c + 1) - 1))
                dve.wait_ge(ud_ready, chunk_no(i, c))
                dve.wait_ge(gate_ready, chunk_no(i, c))
                nc.vector.tensor_tensor(ud[:, c % 2, :], Y, ud[:, c % 2, :], ALU.add).then_inc(y_added, 1)
                dve.wait_ge(y_added, chunk_no(i, c))
                nc.vector.tensor_tensor(ud[:, c % 2, :], ud[:, c % 2, :], gate[:, c % NGATE, :],
                                        ALU.mult).then_inc(y_gated, 1)

            def step(i, s, first=False, final=False):
                loop = None if first else loop_block[0]
                c, g = divmod(s, SPC)
                if g == 0:
                    states = carry[:, c * N:(c + 1) * N]
                    link(nc.vector.tensor_scalar(states, states, limit(lim0, i), limit(lim0 + nlim, i), ALU.min,
                                                 ALU.max), loop)
                if g == 3 and not (first and c == 0):
                    gated_y(i, c - 1)
                dve.wait_ge(exp_done, step_no(i, s))
                dve.wait_ge(dbu_done, step_no(i, s))
                before = not first or s >= 1
                for k in range(PAIR):
                    if k == 1 and before:
                        keep_state(i, s - 1).then_inc(vec_link, 1)
                        links[loop is not None] += 1
                        mark = links[loop is not None]
                    n = c * N + g * PAIR + k
                    last = nc.vector.tensor_tensor_scan(hb[:, HB_SLOT[s], k, :], dA[:, DA_SLOT[s], k, :],
                                                        hb[:, HB_SLOT[s], k, :], carry[:, n:n + 1],
                                                        ALU.mult, ALU.add)
                last.then_inc(scan_done, 1)
                if before:
                    dve.wait_ge(vec_link, mark if loop is None else VEC_LINKS * loop + (links[0] + mark))
                    times_c(i, s - 1)
                mlp(i, s)
                for q in at(DTZ_STEP, s - 4):
                    delta_pair(NC // 2 * i + (q + 1), q + 1)
                if g == 5 and c < NC - 1:
                    du_rows(c + 1, NC * i + (c + 1), NC // 2 * i + (c + 1) // 2)
                if s == LN_STEP and not final:
                    ln_statistics(i, i + 1)
                if s == LN_STEP + 2 and not final:
                    ln_bias(i + 1)
                if s == HEAD - 1 and not first:
                    add_rows(i)
                if s >= HEAD and not final:
                    front(i, i + 1, s)
                if s - STEPS >= EARLY and not final:
                    mlp(i + 1, s - STEPS)

            for s in range(XT_STEP[0], STEPS):
                front(None, FIRST, s)
                if s - STEPS >= EARLY:
                    mlp(0, s - STEPS)
            for s in range(HEAD):
                step(0, s, True)
            with dve.Fori(0, LAST) as i:
                links[1] = 0
                loop_block[0] = i
                for s in range(HEAD, STEPS):
                    step(i, s)
                for s in range(HEAD):
                    step(i + 1, s)
            assert links[1] == VEC_LINKS, links
            links[1], loop_block[0] = 0, LAST
            for s in range(HEAD, STEPS):
                step(LAST, s, final=True)
            link(keep_state(LAST, STEPS - 1), LAST)
            times_c(LAST, STEPS - 1)
            gated_y(BLOCKS, -1)
            add_rows(BLOCKS)


_INS = ["L0_attn_hidden_states", "L0_attn_W_in", "L0_attn_conv_w", "L0_attn_conv_b", "L0_attn_Wx",
        "L0_attn_dt_ln_w", "L0_attn_b_ln_w", "L0_attn_c_ln_w", "L0_attn_Wdt", "L0_attn_dt_bias", "L0_attn_A",
        "L0_attn_D_param", "L0_attn_W_out", "L0_ffn_qweight_gu", "L0_ffn_qzeros_gu", "L0_ffn_scales_gu",
        "L0_ffn_g_idx_gu", "L0_ffn_qweight_down", "L0_ffn_qzeros_down", "L0_ffn_scales_down",
        "L0_ffn_g_idx_down"]


def constants(batch, length):
    import numpy as np

    per = length // T
    blocks = batch * per
    mean = np.zeros((P, P), np.float32)
    for lo, hi in ((0, R), (R, R + N), (R + N, XP)):
        mean[lo:hi, lo:hi] = 1.0 / (hi - lo)
    limits = [0.0 if m % per == 0 else 3.0e38 for m in range(blocks)]
    cols = [np.eye(P, dtype=np.float32), mean, np.arange(P, dtype=np.float32)[:, None],
            np.full((P, 1), -0.5, np.float32), np.full((P, 1), EPS_RMS, np.float32)]
    cols += [np.tile(np.array([v], np.float32), (P, 1)) for v in limits + [-v for v in limits]]
    return np.concatenate(cols, axis=1)


def kernel(**inputs):
    import concourse.bacc as bacc
    import numpy as np
    from concourse.bass_utils import run_bass_kernel_spmd

    nc = bacc.Bacc("TRN2", target_bir_lowering=False, num_devices=1, dynamic_dma_scratch_size=1024)
    arrays, args = {}, []
    for name in _INS:
        a = np.ascontiguousarray(inputs[name])
        arrays[name] = a
        args.append(nc.dram_tensor(name, a.shape, mybir.dt.from_np(a.dtype), kind="ExternalInput").ap())
    shape = arrays[_INS[0]].shape
    arrays["consts"] = constants(shape[0], shape[1])
    args.append(nc.dram_tensor("consts", arrays["consts"].shape, F32, kind="ExternalInput").ap())
    args.append(nc.dram_tensor("out", shape, F32, kind="ExternalOutput").ap())
    build(nc, *args)
    r = run_bass_kernel_spmd(nc, [arrays], core_ids=[0])
    return r.results[0]["out"]
```
